# Optimizing a Trainium2 kernel written in Bass

```python
import numpy as np
import jax
import jax.numpy as jnp

def _softmax(x, axis=-1):
    return jax.nn.softmax(x, axis=axis)

def _gelu(x):
    return jax.nn.gelu(x, approximate=True)

def _silu(x):
    return jax.nn.silu(x)

def _sigmoid(x):
    return jax.nn.sigmoid(x)

def _layernorm(x, axis=-1, eps=1e-05):
    m = jnp.mean(x, axis=axis, keepdims=True)
    v = jnp.var(x, axis=axis, keepdims=True)
    return (x - m) / jnp.sqrt(v + eps)

def _scatter_add(tgt, idx, src, axis=0):
    return tgt.at[idx].add(src)

def _segment_sum(src, seg, n):
    return jax.ops.segment_sum(src, seg, n)
kernel_name = 'mk_macaron_d1_jaxref_r8_3e8491'

def setup_inputs(seed: int=0):
    np.random.seed(seed)
    _w = jnp.asarray

    def _L0_attn_setup():
        import jax, jax.numpy as jnp
        import numpy as np
        TOPK = 32
        NEG = -1e+30

        def hadamard(x):
            d = x.shape[-1]
            shape = x.shape
            x = x.reshape(-1, d)
            h = 1
            while h < d:
                x = x.reshape(-1, d // (2 * h), 2, h)
                a, b = (x[:, :, 0, :], x[:, :, 1, :])
                x = jnp.stack([a + b, a - b], axis=2).reshape(-1, d)
                h *= 2
            return (x * d ** (-0.5)).reshape(shape)
        key = jax.random.key(seed)
        ks = jax.random.split(key, 8)
        D, S, B = (256, 256, 1)
        Hi, Di, H, hd = (16, 128, 16, 128)
        w = 0.02
        return {'x': jax.random.normal(ks[0], (B, S, D), jnp.float32), 'wq_idx': jax.random.normal(ks[1], (D, Hi * Di), jnp.float32) * w, 'wk_idx': jax.random.normal(ks[2], (D, Di), jnp.float32) * w, 'w_iw': jax.random.normal(ks[3], (D, Hi), jnp.float32) * w, 'wq': jax.random.normal(ks[4], (D, H * hd), jnp.float32) * w, 'wk': jax.random.normal(ks[5], (D, hd), jnp.float32) * w, 'wv': jax.random.normal(ks[6], (D, hd), jnp.float32) * w, 'wo': jax.random.normal(ks[7], (H * hd, D), jnp.float32) * w}
    _L0_attn_in = _L0_attn_setup()

    def _L0_ffn_setup():
        import jax, jax.numpy as jnp
        import numpy as np
        B, S, D = (4, 64, 256)
        E, K, H = (8, 2, 176)
        HS = 2 * 176
        ALPHA = 0.001
        W_SCALE = 0.02

        def _moe_forward(hidden_states, gate_w, w_gate, w_up, w_down, sw_gate, sw_up, sw_down):
            b, s, d = hidden_states.shape
            x = hidden_states.reshape(-1, d)
            T = x.shape[0]
            logits = x @ gate_w
            scores = jax.nn.softmax(logits, axis=-1)
            topk_w, topk_idx = jax.lax.top_k(scores, K)
            mask = jax.nn.one_hot(topk_idx, E, dtype=scores.dtype).sum(axis=1)
            ce = mask.mean(axis=0)
            Pi = scores.mean(axis=0)
            aux_loss = (Pi * ce * E).sum() * ALPHA
            comb = jnp.zeros((T, E), dtype=x.dtype)
            comb = comb.at[jnp.arange(T)[:, None], topk_idx].add(topk_w)
            g = jax.nn.silu(jnp.einsum('td,edh->teh', x, w_gate)) * jnp.einsum('td,edh->teh', x, w_up)
            routed = jnp.einsum('teh,ehd,te->td', g, w_down, comb)
            shared = jax.nn.silu(x @ sw_gate) * (x @ sw_up) @ sw_down
            out = (routed + shared).reshape(b, s, d)
            return (out, aux_loss)
        key = jax.random.key(seed)
        ks = jax.random.split(key, 8)
        rn = lambda k, sh: jax.random.normal(k, sh, dtype=jnp.float32)
        return {'hidden_states': rn(ks[0], (B, S, D)), 'gate_w': rn(ks[1], (D, E)) * W_SCALE, 'w_gate': rn(ks[2], (E, D, H)) * W_SCALE, 'w_up': rn(ks[3], (E, D, H)) * W_SCALE, 'w_down': rn(ks[4], (E, H, D)) * W_SCALE, 'sw_gate': rn(ks[5], (D, HS)) * W_SCALE, 'sw_up': rn(ks[6], (D, HS)) * W_SCALE, 'sw_down': rn(ks[7], (HS, D)) * W_SCALE}
    _L0_ffn_in = _L0_ffn_setup()
    _d = {'L0_attn_x': _L0_attn_in['x'], 'L0_attn_wq_idx': _L0_attn_in['wq_idx'], 'L0_attn_wk_idx': _L0_attn_in['wk_idx'], 'L0_attn_w_iw': _L0_attn_in['w_iw'], 'L0_attn_wq': _L0_attn_in['wq'], 'L0_attn_wk': _L0_attn_in['wk'], 'L0_attn_wv': _L0_attn_in['wv'], 'L0_attn_wo': _L0_attn_in['wo'], 'L0_ffn_gate_w': _L0_ffn_in['gate_w'], 'L0_ffn_w_gate': _L0_ffn_in['w_gate'], 'L0_ffn_w_up': _L0_ffn_in['w_up'], 'L0_ffn_w_down': _L0_ffn_in['w_down'], 'L0_ffn_sw_gate': _L0_ffn_in['sw_gate'], 'L0_ffn_sw_up': _L0_ffn_in['sw_up'], 'L0_ffn_sw_down': _L0_ffn_in['sw_down']}
    _x0 = _d['L0_attn_x']
    _d['L0_attn_x'] = jax.random.normal(jax.random.fold_in(jax.random.key(seed), 1), (8, 256, 256), dtype=_x0.dtype)
    del _x0
    return _d

def reference(L0_attn_x, L0_attn_wq_idx, L0_attn_wk_idx, L0_attn_w_iw, L0_attn_wq, L0_attn_wk, L0_attn_wv, L0_attn_wo, L0_ffn_gate_w, L0_ffn_w_gate, L0_ffn_w_up, L0_ffn_w_down, L0_ffn_sw_gate, L0_ffn_sw_up, L0_ffn_sw_down):

    def _L0_attn_ref(x, wq_idx, wk_idx, w_iw, wq, wk, wv, wo):
        import jax, jax.numpy as jnp
        import numpy as np
        TOPK = 32
        NEG = -1e+30

        def hadamard(x):
            d = x.shape[-1]
            shape = x.shape
            x = x.reshape(-1, d)
            h = 1
            while h < d:
                x = x.reshape(-1, d // (2 * h), 2, h)
                a, b = (x[:, :, 0, :], x[:, :, 1, :])
                x = jnp.stack([a + b, a - b], axis=2).reshape(-1, d)
                h *= 2
            return (x * d ** (-0.5)).reshape(shape)
        B, S, D = x.shape
        Di = wk_idx.shape[-1]
        Hi = w_iw.shape[-1]
        hd = wk.shape[-1]
        H = wq.shape[-1] // hd
        qi = hadamard((x @ wq_idx).reshape(B, S, Hi, Di))
        ki = hadamard(x @ wk_idx)
        iw = x @ w_iw
        logits = jax.nn.relu(jnp.einsum('bthd,bsd->bhts', qi, ki))
        I = jnp.einsum('bth,bhts->bts', iw, logits)
        t = jnp.arange(S)
        causal = t[None, :, None] >= t[None, None, :]
        I = jnp.where(causal, I, NEG)
        vals, idx = jax.lax.top_k(I, TOPK)
        valid = vals > NEG / 2
        q = (x @ wq).reshape(B, S, H, hd)
        k = x @ wk
        v = x @ wv
        gather = jax.vmap(lambda kk, ii: kk[ii])
        k_sel, v_sel = (gather(k, idx), gather(v, idx))
        scores = jnp.einsum('bthd,btkd->bhtk', q, k_sel) * hd ** (-0.5)
        scores = jnp.where(valid[:, None], scores, NEG)
        p = jax.nn.softmax(scores, axis=-1)
        o = jnp.einsum('bhtk,btkd->bthd', p, v_sel)
        return o.reshape(B, S, H * hd) @ wo

    def _L0_ffn_ref(hidden_states, gate_w, w_gate, w_up, w_down, sw_gate, sw_up, sw_down):
        import jax, jax.numpy as jnp
        import numpy as np
        B, S, D = (4, 64, 256)
        E, K, H = (8, 2, 176)
        HS = 2 * 176
        ALPHA = 0.001
        W_SCALE = 0.02

        def _moe_forward(hidden_states, gate_w, w_gate, w_up, w_down, sw_gate, sw_up, sw_down):
            b, s, d = hidden_states.shape
            x = hidden_states.reshape(-1, d)
            T = x.shape[0]
            logits = x @ gate_w
            scores = jax.nn.softmax(logits, axis=-1)
            topk_w, topk_idx = jax.lax.top_k(scores, K)
            mask = jax.nn.one_hot(topk_idx, E, dtype=scores.dtype).sum(axis=1)
            ce = mask.mean(axis=0)
            Pi = scores.mean(axis=0)
            aux_loss = (Pi * ce * E).sum() * ALPHA
            comb = jnp.zeros((T, E), dtype=x.dtype)
            comb = comb.at[jnp.arange(T)[:, None], topk_idx].add(topk_w)
            g = jax.nn.silu(jnp.einsum('td,edh->teh', x, w_gate)) * jnp.einsum('td,edh->teh', x, w_up)
            routed = jnp.einsum('teh,ehd,te->td', g, w_down, comb)
            shared = jax.nn.silu(x @ sw_gate) * (x @ sw_up) @ sw_down
            out = (routed + shared).reshape(b, s, d)
            return (out, aux_loss)
        out, _aux = _moe_forward(hidden_states, gate_w, w_gate, w_up, w_down, sw_gate, sw_up, sw_down)
        return out
    x = L0_attn_x
    x = x + 0.5 * _L0_ffn_ref(_layernorm(x, axis=-1), L0_ffn_gate_w, L0_ffn_w_gate, L0_ffn_w_up, L0_ffn_w_down, L0_ffn_sw_gate, L0_ffn_sw_up, L0_ffn_sw_down)
    x = x + _L0_attn_ref(_layernorm(x, axis=-1), L0_attn_wq_idx, L0_attn_wk_idx, L0_attn_w_iw, L0_attn_wq, L0_attn_wk, L0_attn_wv, L0_attn_wo)
    x = x + 0.5 * _L0_ffn_ref(_layernorm(x, axis=-1), L0_ffn_gate_w, L0_ffn_w_gate, L0_ffn_w_up, L0_ffn_w_down, L0_ffn_sw_gate, L0_ffn_sw_up, L0_ffn_sw_down)
    return x

_drawn_inputs = setup_inputs


def setup_inputs(seed=0):
    import zlib

    import numpy as np

    out = dict(_drawn_inputs(seed))
    spreads = {}
    factors = {'L0_attn_wq': 8.0,
     'L0_attn_wk': 8.0,
     'L0_ffn_gate_w': 8.0,
     'L0_ffn_w_gate': 8.0,
     'L0_ffn_w_up': 8.0,
     'L0_ffn_w_down': 8.0,
     'L0_ffn_sw_gate': 2.748,
     'L0_ffn_sw_up': 2.726,
     'L0_ffn_sw_down': 2.718}
    for name, (base, spread) in spreads.items():
        noise = np.random.default_rng([zlib.crc32(name.encode()), seed]).standard_normal(out[name].shape)
        drawn = base * np.exp(spread * noise) if base else spread * noise
        out[name] = jnp.asarray(drawn.astype(out[name].dtype))
    for name, factor in factors.items():
        out[name] = (out[name] * factor).astype(out[name].dtype)
    return out
```

```python
import numpy as np
import concourse.bass as bass
import concourse.mybir as mybir
from contextlib import ExitStack

T = 2048
D = 256
NG = 4
GT = 512
NH = 16
NE = 8
HE = 176
NC = 14
ORDER = [11, 12, 13, 0, 1, 2, 3, 4, 5, 6, 7, 8, 9, 10]
NEG = -1e30
MARK = -3e38
SCALE = float(128) ** -0.5
EPS = 1e-5


def segments(c):
    out, at = [], 128 * c
    while at < 128 * (c + 1):
        e = at // HE
        end = min(128 * (c + 1), HE * (e + 1))
        out.append((at - 128 * c, end - at, e))
        at = end
    return out


def macaron_kernel(nc, x, ident_in, less_in, gw_in, wf_in, wqi_in, ws_in, wiw_in, wq_in, wo_in, out):
    f32 = mybir.dt.float32
    f32r = mybir.dt.float32r
    i32 = mybir.dt.int32
    ALU = mybir.AluOpType
    ACT = mybir.ActivationFunctionType
    AX = mybir.AxisListType

    ctx = ExitStack()
    with ctx:
        def sb(name, shape, dt=f32, stack=ctx):
            return stack.enter_context(nc.sbuf_tensor(name, shape, dt))

        X = sb("X", [128, 16, D])
        R1 = sb("R1", [128, 21504], f32r)
        R2 = sb("R2", [128, 9728], f32r)
        stage = sb("stage", [128, 2, 768])
        xf = sb("xf", [128, 2, GT])
        xh = sb("xh", [128, 2, 2, GT], f32r)
        xl = sb("xl", [128, 2, 2, GT], f32r)
        ident = sb("ident", [128, 128])
        gw = sb("gw", [128, 2, NE])
        wiw = sb("wiw", [128, 2, NH])
        st = sb("st", [128, 4, 6])
        mv = sb("mv", [128, 4, 2])
        nt = sb("nt", [128, 4, 4])
        PS = [ctx.enter_context(nc.psum_tensor(f"ps{i}", [128, 512], f32)) for i in range(8)]
        scratch = nc.dram_tensor("comb_scratch", [2 * NG, 32, 128], f32, kind="Internal").ap()

        prog = {e: [] for e in ("pe", "act", "dve", "pool", "sp")}
        count = {}

        def op(eng, fn, waits=(), sem=None):
            inc = 16 if eng == "sp" else 1
            if sem is None:
                sem = eng
            count[sem] = count.get(sem, 0) + inc
            prog[eng].append((fn, list(waits), sem, inc))
            return (sem, count[sem])

        def quiet(eng, fn, waits=()):
            prog[eng].append((fn, list(waits), None, 0))

        def pe(sem, waits, mms):
            for n, (o, l, r, start, stop) in enumerate(mms):
                def fn(e, o=o, l=l, r=r, start=start, stop=stop):
                    return e.matmul(o, l, r, start=start, stop=stop, skip_group_check=True)
                w = waits if n == 0 else ()
                if n == len(mms) - 1:
                    return op("pe", fn, w, sem)
                quiet("pe", fn, w)

        def three(o, pairs, first=True, last=True):
            seq = [q for lh, ll, rh, rl in pairs for q in ((lh, rh), (lh, rl), (ll, rh))]
            return [(o, a, b, first and i == 0, last and i == len(seq) - 1) for i, (a, b) in enumerate(seq)]

        def f(ap):
            return ap.bitcast(f32)

        def copy(eng, o, i, waits, sem=None):
            if eng == "act":
                return op("act", lambda e: e.activation(o, i, ACT.Copy), waits, sem)
            return op(eng, lambda e: e.tensor_copy(o, i), waits, sem)

        def tt(eng, o, a, b, alu, waits, sem=None):
            return op(eng, lambda e: e.tensor_tensor(o, a, b, alu), waits, sem)

        def load(dst, src, waits, sem):
            return op("sp", lambda e: e.dma_start(dst, src), waits, sem)

        XT = [None] * NG
        XT[0] = load(X[:, 0:4, :], x[0:512, :].rearrange("(t p) d -> p t d", p=128), [], "x0")
        t_id = load(ident[:], ident_in, [], "c0")
        t_gw = load(gw[:], gw_in.rearrange("p (c e) -> p c e", c=2), [], "c1")

        stage_free = [[], []]
        nst = [0]

        def weight(src, n, dst, waits=()):
            s = nst[0] % 2
            nst[0] += 1
            t = load(stage[:, s, 0:n], src, stage_free[s], f"w{s}")
            hi, lo = dst[:, 0:n], dst[:, n:2 * n]
            a = copy("pool", hi, stage[:, s, 0:n], [t, *waits], "split")
            b = tt("pool", lo, stage[:, s, 0:n], f(hi), ALU.subtract, [a], "split")
            stage_free[s] = [b]
            return b

        def rsqrt(v, w0):
            a, y, b = nt[:, :, 0], nt[:, :, 3], nt[:, :, 1]
            t = op("dve", lambda e: e.tensor_scalar(a, v, EPS, None, ALU.add), w0)
            t = op("dve", lambda e: e.tensor_scalar(b.bitcast(i32), a.bitcast(i32), 1, None,
                                                    ALU.logical_shift_right), [t])
            t = op("dve", lambda e: e.tensor_scalar(y.bitcast(i32), b.bitcast(i32), -1.0, float(0x5f3759df),
                                                    ALU.mult, ALU.add), [t])
            for _ in range(4):
                t = tt("dve", b, y, y, ALU.mult, [t])
                t = op("dve", lambda e: e.scalar_tensor_tensor(b, b, -0.5, a, ALU.mult, ALU.mult), [t])
                t = op("dve", lambda e: e.scalar_tensor_tensor(y, b, 1.5, y, ALU.add, ALU.mult), [t])
            return t

        def norm(g, ready, xn, xn_free):
            ts = []
            for i in range(4):
                t = op("dve", lambda e, i=i: e.bn_stats(st[:, i, :], X[:, 4 * g + i, :]), ready if i == 0 else [])
            for i in range(4):
                t = op("dve", lambda e, i=i: e.bn_aggr(mv[:, i, :], st[:, i, :]), [t] if i == 0 else [])
            t = rsqrt(mv[:, :, 1], [t])
            for i in range(4):
                t = op("dve", lambda e, i=i: e.tensor_scalar(xn[:, i, :], X[:, 4 * g + i, :], mv[:, i, 0:1],
                                                             nt[:, i, 3:4], ALU.subtract, ALU.mult),
                       [t] + xn_free if i == 0 else [], "xn")
            return t

        xbuf_free = [[], []]

        def flip(g, xn, t_xn, banks, bank_free):
            pts = []
            for dc in range(2):
                for i in range(4):
                    o, s = PS[banks[dc]][:, 128 * i:128 * i + 128], xn[:, i, 128 * dc:128 * dc + 128]
                    fn = lambda e, o=o, s=s: e.transpose(o, s, ident[:])
                    w = ([t_xn, t_id] if dc == 0 else []) + bank_free[dc] if i == 0 else []
                    if i == 3:
                        pts.append(op("pe", fn, w, "pe_xt"))
                    else:
                        quiet("pe", fn, w)
            b = g % 2
            for dc in range(2):
                ta = copy("act", xf[:, dc, :], PS[banks[dc]][:, :], [pts[1]], "xf")
            th = copy("dve", xh[:, b, :, :], xf[:, :, :], [ta] + xbuf_free[b], "xh")
            tl = tt("dve", xl[:, b, :, :], xf[:, :, :], f(xh[:, b, :, :]), ALU.subtract, [th], "xl")
            return ta, th, tl, pts[1]

        def ffn(n, res_ready, slots, wt, on_group, tail_loads):
            xn = xf[:, :, :].rearrange("p c (t d) -> p (c t) d", d=D)
            S = sb(f"S{n}", [128, 2, GT], f32, fs)
            TM = sb(f"TM{n}", [128, 2, GT], f32, fs)
            GH = sb(f"GH{n}", [128, 3, GT], f32r, fs)
            GL = sb(f"GL{n}", [128, 3, GT], f32r, fs)
            CB = sb(f"CB{n}", [128, 4, GT], f32, fs)
            LG = sb(f"LG{n}", [128, 4, NE], f32, fs)
            EX = sb(f"EX{n}", [128, 4, NE], f32, fs)
            G1 = sb(f"G1{n}", [128, 4, NE * NE], f32, fs)
            G2 = sb(f"G2{n}", [128, 4, NE * NE], f32, fs)
            less = sb(f"less{n}", [128, NE * NE], f32, fs)
            RK = sb(f"RK{n}", [128, 4, NE], f32, fs)
            mx = sb(f"mx{n}", [128, 4], f32, fs)
            sm = sb(f"sm{n}", [128, 4], f32, fs)
            CT = sb(f"CT{n}", [32, 128], f32, fs)
            t_less = load(less[:], less_in, tail_loads, "c2")
            free = {k: [] for k in range(8)}
            GB, UB, YB, RB = (0, 1), (2, 3), (4, 5), (6, 7)
            s_free, tm_free, cb_free = [[], []], [[], []], [[] for _ in range(4)]
            gh_free = [[], [], []]
            ncb = [0]
            XR = {}
            comb = {}
            lg_free, ct_free = [[]], [[]]

            def prep(g):
                t = norm(g, res_ready(g), xn, XR[g - 1][4] if g else [])
                ta, th, tl, tp = flip(g, xn, t, RB, [free[6], free[7]])
                free[7] = [ta]
                mms = [(PS[6][:, NE * i:NE * i + NE], xf[:, dc, 128 * i:128 * i + 128], gw[:, dc, :], dc == 0, dc == 1)
                       for i in range(4) for dc in range(2)]
                tg = pe("pe_gate", [ta, t_gw], mms)
                XR[g] = (ta, th, tl, tp, [tg, tl])
                lg = PS[6][:, 0:32].rearrange("p (t e) -> p t e", e=NE)
                t = copy("dve", LG[:], lg, [tg] + lg_free[0])
                free[6] = [t]
                t = op("dve", lambda e: e.tensor_reduce(mx[:], LG[:], AX.X, ALU.max), [t])
                bc = lambda a: a[:, :].rearrange("p (t o) -> p t o", o=1).to_broadcast([128, 4, NE])
                t = tt("dve", EX[:], LG[:], bc(mx), ALU.subtract, [t])
                te = op("act", lambda e: e.activation(EX[:], EX[:], ACT.Exp), [t])
                four = [128, 4, NE, NE]
                j_ = LG[:, :, :].rearrange("p t (o e) -> p t o e", o=1).to_broadcast(four)
                e_ = LG[:, :, :].rearrange("p t (e o) -> p t e o", o=1).to_broadcast(four)
                g4 = lambda a: a[:, :, :].rearrange("p t (e j) -> p t e j", j=NE)
                for q in range(4):
                    jq = LG[:, q, :].rearrange("p (o e) -> p o e", o=1).to_broadcast([128, NE, NE])
                    eq = LG[:, q, :].rearrange("p (e o) -> p e o", o=1).to_broadcast([128, NE, NE])
                    gq = lambda a: a[:, q, :].rearrange("p (e j) -> p e j", j=NE)
                    t1 = tt("dve", gq(G1), jq, eq, ALU.is_gt, [])
                    t2 = tt("dve", gq(G2), jq, eq, ALU.is_ge, [])
                lb = less[:, :].rearrange("p (o n) -> p o n", o=1).to_broadcast([128, 4, NE * NE])
                t2 = tt("dve", G2[:], G2[:], lb, ALU.mult, [t2, t_less])
                t2 = tt("dve", G1[:], G1[:], G2[:], ALU.max, [t2])
                t2 = op("dve", lambda e: e.tensor_reduce(RK[:], g4(G1), AX.X, ALU.add), [t2])
                t = op("dve", lambda e: e.tensor_reduce(sm[:], EX[:], AX.X, ALU.add), [te])
                t = op("dve", lambda e: e.reciprocal(sm[:], sm[:]), [t])
                t = tt("dve", EX[:], EX[:], bc(sm), ALU.mult, [t])
                t = op("dve", lambda e: e.scalar_tensor_tensor(EX[:], RK[:], 2.0, EX[:], ALU.is_lt, ALU.mult), [t])
                lg_free[0] = [t]
                t = pe("pe_gate", [t, t_id] + free[7],
                       [(PS[7][0:32, 0:128], EX[:, :, :].rearrange("p t e -> p (t e)"), ident[:], True, True)])
                t = copy("act", CT[:], PS[7][0:32, 0:128], [t] + ct_free[0])
                free[7] = [t]
                comb[g] = load(scratch[NG * n + g], CT[:], [t], f"cs{g % 2}")
                ct_free[0] = [comb[g]]

            def combine_rows(g, c):
                k = ncb[0] % 4
                ncb[0] += 1
                for i, (p, rows, e) in enumerate(segments(c)):
                    src = scratch[NG * n + g].rearrange("(t e) q -> e t q", e=NE)[e:e + 1, :, :]
                    t = load(CB[p:p + rows, k, :].rearrange("p (t q) -> p t q", q=128),
                             src.to_broadcast([rows, 4, 128]), [comb[g]] + cb_free[k], f"cb{k}")
                return k, t

            prep(0)
            tasks = [(g, i) for g in range(NG) for i in range(NC)]
            cbs = {}
            routed = [(g, i) for g, i in tasks if ORDER[i] < 11]
            down_q = {}

            def down(g, i, tok, k3):
                c = ORDER[i]
                w = slots[c]
                for a in range(4):
                    y = PS[YB[a // 2]][:, 256 * (a % 2):256 * (a % 2) + 256]
                    sl = slice(128 * a, 128 * a + 128)
                    mms = [(y, GH[:, k3, sl], w[:, 512:768]), (y, GH[:, k3, sl], w[:, 1280:1536]),
                           (y, GL[:, k3, sl], w[:, 512:768])]
                    mms = [(*m, i == 0 and a % 2 == 0 and q == 0, i == NC - 1 and q == 2) for q, m in enumerate(mms)]
                    wts = [*tok] if a == 0 else []
                    if i == 0:
                        wts = wts + free[YB[a // 2]]
                    t = pe("pe_down", wts, mms)
                gh_free[k3] = [t]
                if i == NC - 1:
                    for b in range(2):
                        xs = X[:, 4 * g + 2 * b:4 * g + 2 * b + 2, :]
                        y = PS[YB[b]][:, :].rearrange("p (t d) -> p t d", d=D)
                        tx = op("dve", lambda e, xs=xs, y=y: e.scalar_tensor_tensor(xs, y, 0.5, xs, ALU.mult, ALU.add),
                                [t], "xres")
                        free[YB[b]] = [tx]
                    on_group(g, tx)
                return t

            last = None
            for s, (g, i) in enumerate(tasks + [None, None]) if False else enumerate(tasks + [(None, None)] * 2):
                if g is not None:
                    c = ORDER[i]
                    w = slots[c]
                    if i == 0:
                        for r in range(4):
                            cbs[(g, 3 + r)] = combine_rows(g, ORDER[3 + r])
                    ta, th, tl, tp, _ = XR[g]
                    b = g % 2
                    toks = []
                    for z, banks in enumerate((GB, UB)):
                        bk = banks[s % 2]
                        pairs = [(w[:, z * 256 + dc * 128:z * 256 + dc * 128 + 128],
                                  w[:, 768 + z * 256 + dc * 128:768 + z * 256 + dc * 128 + 128],
                                  xh[:, b, dc, :], xl[:, b, dc, :]) for dc in range(2)]
                        toks.append(pe("pe_gu", [th, tl, wt[c]] + free[bk], three(PS[bk][:, :], pairs)))
                    if i == NC - 1:
                        xbuf_free[b] = [toks[1]]
                    k2, k3 = s % 2, s % 3
                    t = op("act", lambda e, k2=k2, gb=GB[s % 2]: e.activation(S[:, k2, :], PS[gb][:, :], ACT.Silu),
                           [toks[0]] + s_free[k2], "silu")
                    free[GB[s % 2]] = [t]
                    t = tt("dve", TM[:, k2, :], S[:, k2, :], PS[UB[s % 2]][:, :], ALU.mult, [t, toks[1]] + tm_free[k2])
                    free[UB[s % 2]] = [t]
                    s_free[k2] = [t]
                    if c < 11:
                        k4, tc = cbs.pop((g, i))
                        t = tt("pool", TM[:, k2, :], TM[:, k2, :], CB[:, k4, :], ALU.mult, [t, tc])
                        cb_free[k4] = [t]
                        if i + 4 < NC:
                            cbs[(g, i + 4)] = combine_rows(g, ORDER[i + 4])
                    t1 = copy("act", GH[:, k3, :], TM[:, k2, :], [t] + gh_free[k3], "gh")
                    t2 = tt("dve", GL[:, k3, :], TM[:, k2, :], f(GH[:, k3, :]), ALU.subtract, [t1, *gh_free[k3]], "gl")
                    tm_free[k2] = [t2]
                    down_q[s] = (g, i, (t1, t2), k3)
                if s - 2 in down_q:
                    last = down(*down_q.pop(s - 2))
                if g is not None and i == 5 and g + 1 < NG:
                    prep(g + 1)
            return free, [last]

        fs = ExitStack()
        slots1 = {c: R1[:, 1536 * c:1536 * c + 1536] for c in range(NC)}
        wt1 = {}
        for n, c in enumerate(ORDER):
            wt1[c] = weight(wf_in[c], 768, slots1[c])
            if n == 2:
                for g in range(1, NG):
                    XT[g] = load(X[:, 4 * g:4 * g + 4, :],
                                 x[512 * g:512 * g + 512, :].rearrange("(t p) d -> p t d", p=128), [], f"x{g}")
        t_iw = load(wiw[:], wiw_in.rearrange("p (c e) -> p c e", c=2), [], "c3")
        t_small = weight(ws_in, 768, R2[:, 8192:9728])
        t_wqi = [weight(wqi_in[k], 512, R2[:, 1024 * k:1024 * k + 1024]) for k in range(8)]
        xres = [None] * NG

        def keep(g, t):
            xres[g] = t

        free1, last1 = ffn(0, lambda g: [XT[g]], slots1, wt1, keep, [])
        fs.close()
        edge = [(s, count[s]) for s in ("pe_down", "dve", "gl", "act", "gh", "pool", "xres")]

        fs = ExitStack()
        A = lambda name, shape, dt=f32: sb(name, shape, dt, fs)
        PTH = R1[:, 16384:17152].rearrange("p (h n) -> p h n", h=2)
        PTL = R1[:, 17152:17920].rearrange("p (h n) -> p h n", h=2)
        OH, OL = R1[:, 17920:18432], R1[:, 18432:18944]
        QIH = R1[:, 18944:19200].rearrange("p (b n) -> p b n", b=2)
        QIL = R1[:, 19200:19456].rearrange("p (b n) -> p b n", b=2)
        QH = R1[:, 19456:20480].rearrange("p (r b n) -> p r b n", r=4, b=2)
        QL = R1[:, 20480:21504].rearrange("p (r b n) -> p r b n", r=4, b=2)
        QIF = A("QIF", [128, 2, 128])
        QF = A("QF", [128, 4, 2, 128])
        KIF = A("KIF", [128, 2, 128])
        KF = A("KF", [128, 2, 128])
        KIH, KIL = A("KIH", [128, GT], f32r), A("KIL", [128, GT], f32r)
        KH, KL = A("KH", [128, GT], f32r), A("KL", [128, GT], f32r)
        VH, VL = A("VH", [128, 2, 4, 128], f32r), A("VL", [128, 2, 4, 128], f32r)
        SP = A("SP", [128, 2, 2, 384])
        R = A("R", [128, 2, 384])
        I = A("I", [128, 768])
        B = A("B", [128, 768])
        IW = A("IW", [128, 4, NH])
        M8 = A("M8", [128, 4, 8])
        MX = A("MX", [128, 2, 4])
        NB = A("NB", [128, 2, 4])
        SM = A("SM", [128, 2, 4])
        RC = A("RC", [128, 2, 4])
        QB, SB_, TB, OB, YB = 0, (1, 2), (3, 4), 5, (6, 7)
        free = {k: list(edge) for k in range(8)}
        t_wq = [weight(wq_in[k], 512, R1[:, 1024 * k:1024 * k + 1024], edge) for k in range(8)]
        t_wo = [weight(wo_in[k], 512, R1[:, 8192 + 1024 * k:8192 + 1024 * k + 1024], edge) for k in range(8)]
        xn = xf[:, :, :].rearrange("p c (t d) -> p (c t) d", d=D)
        xbuf_free[0] = list(edge)
        xbuf_free[1] = list(edge)
        XR, normed = {}, {}
        xn_free = [list(edge)]
        rf = {k: list(edge) for k in ("qi", "ki", "k", "iw", "i", "b", "r0", "r1", "o", "pt", "v0", "v1", "sp0", "sp1",
                                      "q0", "q1", "q2", "q3", "kf")}
        TILES = [(b, h, 384 * b + 128 * h, 128 * (h + 1)) for b in range(2) for h in range(2)]

        def do_norm(g):
            normed[g] = norm(g, [xres[g], *edge], xn, xn_free[0])

        def small(kind, hl, dc):
            o = 8192 + 768 * hl + 256 * kind + 128 * dc
            return R2[:, o:o + 128]

        tk = {}

        def project(kind, g):
            b = g % 2
            _, th, tl, _ = XR[g]
            pairs = [(small(kind, 0, dc), small(kind, 1, dc), xh[:, b, dc, :], xl[:, b, dc, :]) for dc in range(2)]
            t = pe("pe_k", [th, tl, t_small] + free[QB], three(PS[QB][:, :], pairs))
            KX_F, KX_H, KX_L, name = ((KIF, KIH, KIL, "ki"), (KF, KH, KL, "k"))[kind]
            p2 = PS[QB][:, :].rearrange("p (b n) -> p b n", b=2)
            t1 = copy("act", KX_F[:, :, :], p2[:, :, 0:128], [t] + rf[name])
            t2 = copy("act", KX_H[:, :], PS[QB][:, :], rf[name], "kh")
            t3 = tt("dve", KX_L[:, :], PS[QB][:, :], f(KX_H[:, :]), ALU.subtract, [t2] + rf[name], "kl")
            free[QB] = [t3]
            tk[name] = [t1, t2, t3]

        def values(g):
            b = g % 2
            _, th, tl, _ = XR[g]
            ts = []
            for a in range(4):
                bk = TB[a // 2]
                o = PS[bk][:, 256 * (a % 2):256 * (a % 2) + 256]
                seq = []
                for dc in range(2):
                    wv = R2[:, 8192:9728].rearrange("p (l n) -> p l n", l=2)[:, :, 512 + 128 * dc:640 + 128 * dc]
                    for s_ in (xh, xl):
                        seq.append((s_[:, b, dc, 128 * a:128 * a + 128], wv))
                mms = [(o, l, r, n == 0, n == 3) for n, (l, r) in enumerate(seq)]
                ts.append(pe("pe_v", free[bk] if a % 2 == 0 else [], mms))
            vb = b
            vt = SP
            for z in range(2):
                src = PS[TB[z]][:, :].rearrange("p (t l n) -> p t l n", t=2, l=2)
                t1 = copy("act", f(VL[:, vb, 2 * z:2 * z + 2, :]) if False else R[:, 0, 0:256].rearrange("p (t n) -> p t n", t=2),
                          src[:, :, 1, :], [ts[2 * z + 1]] + rf["r0"])
                rv = R[:, 0, 0:256].rearrange("p (t n) -> p t n", t=2)
                t2 = tt("dve", rv, rv, src[:, :, 0, :], ALU.add, [t1])
                free[TB[z]] = [t2]
                t3 = copy("dve", VH[:, vb, 2 * z:2 * z + 2, :], rv, [t2] + rf[f"v{vb}"], "vh")
                t4 = tt("dve", VL[:, vb, 2 * z:2 * z + 2, :], rv, f(VH[:, vb, 2 * z:2 * z + 2, :]), ALU.subtract,
                        [t3], "vl")
                rf["r0"] = [t4]
            tk["v"] = [t3, t4]

        def weights_of_heads(g):
            ta = XR[g][0]
            mms = [(PS[SB_[0]][:, NH * i:NH * i + NH], xf[:, dc, 128 * i:128 * i + 128], wiw[:, dc, :], dc == 0, dc == 1)
                   for i in range(4) for dc in range(2)]
            t = pe("pe_iw", [ta, t_iw] + free[SB_[0]], mms)
            xn_free[0] = [t, XR[g][2]]
            t = copy("dve", IW[:], PS[SB_[0]][:, 0:64].rearrange("p (t e) -> p t e", e=NH), [t] + rf["iw"])
            free[SB_[0]] = [t]
            tk["iw"] = [t]

        def flip_group(g):
            XR[g] = flip(g, xn, normed[g], SB_, [free[SB_[0]], free[SB_[1]]])
            free[SB_[0]] = free[SB_[1]] = [XR[g][0]]

        def topk(g, b):
            for h in range(2):
                o, n = 384 * b + 128 * h, 128 * (h + 1)
                i = 2 * b + h
                Is, Bs = I[:, o:o + n], B[:, o:o + n]
                W = R[:, b, 128 * h:128 * h + n]
                t = op("pool", lambda e, Is=Is, n=n, h=h: e.affine_select(
                    out=Is, in_=Is, compare_op=ALU.is_ge, fill=NEG, base=128 * h, pattern=[[-1, n]],
                    channel_multiplier=1), [tk[f"i{i}"]])
                src = Is
                for r in range(4):
                    t = op("dve", lambda e, src=src, i=i: e.max(M8[:, i, :], src), [t] + (rf[f"r{b}"] if r == 0 else []))
                    t = op("dve", lambda e, src=src, W=W, i=i: e.match_replace(W, M8[:, i, :], src, MARK), [t])
                    src = W
                t = op("dve", lambda e, W=W: e.tensor_scalar(W, W, MARK, None, ALU.not_equal), [t])
                t = op("dve", lambda e, W=W, Is=Is: e.scalar_tensor_tensor(W, Is, NEG / 2, W, ALU.is_le, ALU.max), [t])
                t = op("dve", lambda e, W=W, Bs=Bs: e.tensor_scalar(Bs, W, NEG, None, ALU.mult), [t] + rf["b"])
                tk[f"b{i}"] = t
            rf[f"r{b}"] = [t]

        def head(g, h, wsrc, wtok, F, H, L, wf_, sem):
            b = g % 2
            _, th, tl, _ = XR[g]
            k, i = h // 2, h % 2
            w = wsrc[:, 1024 * k:1024 * k + 1024]
            pairs = [(w[:, 256 * i + 128 * dc:256 * i + 128 * dc + 128],
                      w[:, 512 + 256 * i + 128 * dc:512 + 256 * i + 128 * dc + 128],
                      xh[:, b, dc, :], xl[:, b, dc, :]) for dc in range(2)]
            t = pe(sem, [th, tl, wtok[k]] + free[QB], three(PS[QB][:, :], pairs))
            p2 = PS[QB][:, :].rearrange("p (b z n) -> p b z n", b=2, z=2)
            t1 = copy("act", F, p2[:, :, 0, :], [t] + rf[wf_], sem + "f")
            t2 = copy("act", H, p2[:, :, 1, :], rf[wf_], sem + "h")
            t3 = tt("dve", L, p2[:, :, 1, :], f(H), ALU.subtract, [t2] + rf[wf_], sem + "l")
            free[QB] = [t3]
            if h == NH - 1 and sem == "pe_q":
                xbuf_free[b] = [t]
            return [t1, t2, t3]

        def products(bank, b, F, H, L, KXF, KXH, KXL, waits, sem):
            o = PS[bank]
            kb = slice(256 * b, 256 * b + 256)
            mms = [(o[:, 0:128], F[:, b, :], KXF[:, b, :], True, True)]
            mms += three(o[:, 128:384], [(H[:, b, :], L[:, b, :], KXH[:, kb], KXL[:, kb])])
            return pe(sem, waits + free[bank], mms)

        def idx_project(g, h):
            tk["qi"] = head(g, h, R2, t_wqi, QIF[:, :, :], QIH[:, :, :], QIL[:, :, :], "qi", "pe_qi")

        def idx_logits(g, h):
            for b in range(2):
                t = products(SB_[b], b, QIF, QIH, QIL, KIF, KIH, KIL, tk["qi"] + tk["ki"], "pe_l")
                tr = op("act", lambda e, b=b: e.activation(R[:, b, :], PS[SB_[b]][:, 0:384], ACT.Relu),
                        [t] + rf[f"r{b}"], "relu")
                free[SB_[b]] = [tr]
                for z in range(2):
                    i = 2 * b + z
                    o, n = 384 * b + 128 * z, 128 * (z + 1)
                    r, Is, iw = R[:, b, 128 * z:128 * z + n], I[:, o:o + n], IW[:, i, h:h + 1]
                    if h == 0:
                        ta = op("dve", lambda e, r=r, Is=Is, iw=iw: e.tensor_scalar(Is, r, iw, None, ALU.mult),
                                [tr, *tk["iw"]] + rf["i"], "acc")
                    else:
                        ta = op("dve", lambda e, r=r, Is=Is, iw=iw: e.scalar_tensor_tensor(
                            Is, r, iw, Is, ALU.mult, ALU.add), [tr, tk[f"i{i}"]], "acc")
                    tk[f"i{i}"] = ta
                rf[f"r{b}"] = [ta]
            rf["qi"] = [t]
            if h == NH - 1:
                rf["ki"] = [t]
                rf["iw"] = [ta]

        qt = {}
        SMT, PTT, OT, YT = {}, {}, {}, {}

        def main_project(U):
            g, u = divmod(U, 16)
            r = u % 4
            qt[U] = head(g, u, R1, t_wq, QF[:, r, :, :], QH[:, r, :, :], QL[:, r, :, :], f"q{r}", "pe_q")

        def scores(U):
            g, u = divmod(U, 16)
            j, b = divmod(u, 2)
            k = U % 2
            for i in range(2):
                h = 2 * j + i
                r = h % 4
                t = products(SB_[i], b, QF[:, r, :, :], QH[:, r, :, :], QL[:, r, :, :], KF, KH, KL,
                             qt[16 * g + h] + tk["k"], "pe_s")
                if b == 1:
                    rf[f"q{r}"] = [t]
                for z in range(2):
                    n, o = 128 * (z + 1), 128 * z
                    tm = op("dve", lambda e, i=i, z=z, n=n, o=o, k=k, b=b: e.tensor_tensor_reduce(
                        out=SP[:, k, i, o:o + n], in0=PS[SB_[i]][:, o:o + n], in1=B[:, 384 * b + o:384 * b + o + n],
                        scale=1.0, scalar=-3e38, op0=ALU.add, op1=ALU.max, accum_out=MX[:, k, 2 * i + z:2 * i + z + 1]),
                        [t, tk[f"b{2 * b + z}"]] + rf[f"sp{k}"], "mask")
                free[SB_[i]] = [tm]
            tn = op("dve", lambda e, k=k: e.tensor_scalar(NB[:, k, :], MX[:, k, :], -SCALE, None, ALU.mult), [tm], "nb")
            for i in range(2):
                for z in range(2):
                    n, o = 128 * (z + 1), 128 * z
                    te = op("act", lambda e, i=i, z=z, n=n, o=o, k=k: e.activation(
                        SP[:, k, i, o:o + n], SP[:, k, i, o:o + n], ACT.Exp, scale=SCALE,
                        bias=NB[:, k, 2 * i + z:2 * i + z + 1], accum_out=SM[:, k, 2 * i + z:2 * i + z + 1]),
                        [tn], "exp")
            SMT[U] = te
            if u == 15:
                rf["k"] = [t]
                rf["b"] = [tm]

        def normalise(U):
            k = U % 2
            t = op("dve", lambda e, k=k: e.reciprocal(RC[:, k, :], SM[:, k, :]), [SMT[U]], "rc")
            for i in range(2):
                for z in range(2):
                    n, o = 128 * (z + 1), 128 * z
                    t = op("pool", lambda e, i=i, z=z, n=n, o=o, k=k: e.tensor_scalar(
                        SP[:, k, i, o:o + n], SP[:, k, i, o:o + n], RC[:, k, 2 * i + z:2 * i + z + 1], None, ALU.mult),
                        [t], "pn")
            SMT[U] = t

        def flip_p(U):
            k = U % 2
            for i in range(2):
                o = PS[TB[i]]
                srcs = [SP[:, k, i, 0:128], SP[:, k, i, 128:256], SP[:, k, i, 256:384]]
                for z, s_ in enumerate(srcs):
                    fn = lambda e, o=o, z=z, s_=s_: e.transpose(o[:, 128 * z:128 * z + 128], s_, ident[:])
                    w = [SMT[U]] + free[TB[i]] if z == 0 else []
                    if z == 2:
                        t = op("pe", fn, w, "pe_t")
                    else:
                        quiet("pe", fn, w)
                th = copy("act", PTH[:, i, :], o[:, 0:384], [t] + rf["pt"], "pth")
                tl = tt("dve", PTL[:, i, :], o[:, 0:384], f(PTH[:, i, :]), ALU.subtract, [th] + rf["pt"], "ptl")
                free[TB[i]] = [tl]
            rf[f"sp{k}"] = [t]
            PTT[U] = [th, tl]

        def pv(U):
            g, u = divmod(U, 16)
            b = u % 2
            vb = g % 2
            o = PS[OB]
            o2 = o[:, :].rearrange("p (h n) -> p h n", h=2)
            mms = []
            mms += three(o2[:, :, :], [(VH[:, vb, 2 * b, :], VL[:, vb, 2 * b, :], PTH[:, :, 0:256], PTL[:, :, 0:256])],
                         True, False)
            mms += three(o2[:, :, 128:256], [(VH[:, vb, 2 * b + 1, :], VL[:, vb, 2 * b + 1, :],
                                              PTH[:, :, 256:384], PTL[:, :, 256:384])], False, True)
            t = pe("pe_o", PTT[U] + tk[f"v_{g}"] + free[OB], mms)
            rf["pt"] = [t]
            if u == 15:
                rf[f"v{vb}"] = [t]
            th = copy("dve", OH, o[:, :], [t] + rf["o"], "oh")
            tl = tt("dve", OL, o[:, :], f(OH), ALU.subtract, [th], "ol")
            free[OB] = [tl]
            OT[U] = [th, tl]

        outs = []

        def wo(U):
            g, u = divmod(U, 16)
            j, b = divmod(u, 2)
            bank = YB[b]
            first = True
            for i in range(2):
                h = 2 * j + i
                w = R1[:, 8192 + 1024 * (h // 2):8192 + 1024 * (h // 2) + 1024]
                wh, wl = w[:, 256 * (h % 2):256 * (h % 2) + 256], w[:, 512 + 256 * (h % 2):512 + 256 * (h % 2) + 256]
                for z in range(2):
                    sl = slice(256 * i + 128 * z, 256 * i + 128 * z + 128)
                    y = PS[bank][:, 256 * z:256 * z + 256]
                    mms = [(y, OH[:, sl], wh), (y, OH[:, sl], wl), (y, OL[:, sl], wh)]
                    mms = [(*m, j == 0 and i == 0 and z == 0 and q == 0, j == 7 and i == 1 and q == 2)
                           for q, m in enumerate(mms)]
                    wts = OT[U] + [t_wo[h // 2]] if i == 0 and z == 0 else []
                    if j == 0 and first:
                        wts = wts + free[bank]
                    first = False
                    t = pe("pe_y", wts, mms)
            rf["o"] = [t]
            if j == 7:
                xs = X[:, 4 * g + 2 * b:4 * g + 2 * b + 2, :]
                y = PS[bank][:, :].rearrange("p (t d) -> p t d", d=D)
                tx = tt("dve", xs, xs, y, ALU.add, [t], "xres")
                free[bank] = [tx]
                xres[g] = tx

        do_norm(0)
        flip_group(0)
        project(0, 0)
        weights_of_heads(0)
        do_norm(1)
        idx_project(0, 0)
        for h in range(NH):
            idx_logits(0, h)
            if h + 1 < NH:
                idx_project(0, h + 1)
        for g in range(NG):
            project(1, g)
            values(g)
            tk[f"v_{g}"] = tk["v"]
            topk(g, 0)
            main_project(16 * g)
            main_project(16 * g + 1)
            topk(g, 1)
            rf["i"] = [tk[f"b{3}"]]
            if g + 1 < NG:
                flip_group(g + 1)
                project(0, g + 1)
                weights_of_heads(g + 1)
            for u in range(16):
                U = 16 * g + u
                if g + 1 < NG:
                    idx_project(g + 1, u)
                scores(U)
                if U >= 3:
                    wo(U - 3)
                if U >= 2:
                    pv(U - 2)
                if U >= 1:
                    flip_p(U - 1)
                if u + 2 < 16:
                    main_project(U + 2)
                if g + 1 < NG:
                    idx_logits(g + 1, u)
                normalise(U)
                if u == 8 and g + 2 < NG:
                    do_norm(g + 2)
            if g == NG - 2:
                r2_edge = [(s, count[s]) for s in ("pe_qi", "pe_k", "pe_v")]
        for U in (64, 65, 66):
            wo(U - 3)
            if U < 66:
                pv(U - 2)
            if U < 65:
                flip_p(U - 1)
        fs.close()
        edge2 = [(s, count[s]) for s in ("pe_y", "pe_o", "dve", "ol", "act", "pth", "pn", "xres", "exp")]

        fs = ExitStack()
        slots2, wt2 = {}, {}
        r2_edge += [(s, count[s]) for s in ("pe_k", "pe_v")]
        for n, c in enumerate(ORDER):
            if n < 6:
                slots2[c] = R2[:, 1536 * n:1536 * n + 1536]
                wt2[c] = weight(wf_in[c], 768, slots2[c], r2_edge)
            else:
                slots2[c] = R1[:, 1536 * (n - 6):1536 * (n - 6) + 1536]
                wt2[c] = weight(wf_in[c], 768, slots2[c], edge2)
        xbuf_free[0] = list(edge2)
        xbuf_free[1] = list(edge2)

        def store(g, t):
            outs.append(load(out[512 * g:512 * g + 512, :].rearrange("(t p) d -> p t d", p=128),
                             X[:, 4 * g:4 * g + 4, :], [t], f"out{g}"))

        ffn(1, lambda g: [xres[g], *edge2], slots2, wt2, store, edge2)
        fs.close()

        sems = {s: ctx.enter_context(nc.semaphore(f"s_{s}")) for s in count}
        block = ctx.enter_context(nc.Block())

        def run(e, name):
            seen = {}
            for fn, waits, sem, inc in prog[name]:
                for s, v in waits:
                    if seen.get(s, 0) < v:
                        e.wait_ge(sems[s], v)
                        seen[s] = v
                ins = fn(e)
                if sem is not None:
                    ins.then_inc(sems[sem], inc)

        @block.tensor
        def _(e):
            run(e, "pe")

        @block.scalar
        def _(e):
            run(e, "act")

        @block.vector
        def _(e):
            run(e, "dve")

        @block.gpsimd
        def _(e):
            run(e, "pool")

        @block.sync
        def _(e):
            run(e, "sp")
            for s, v in outs:
                e.wait_ge(sems[s], v)


def kernel(**inputs):
    import numpy as _np
    import concourse.bacc as _bacc
    from concourse import mybir as _mybir
    from concourse.bass_utils import run_bass_kernel_spmd as _run

    a = {k[3:]: _np.asarray(v) for k, v in inputs.items()}

    def halves(w):
        return w.reshape(2, 128, w.shape[1]).transpose(1, 0, 2)

    def chunked(w, s):
        w = _np.concatenate([w.transpose(1, 0, 2).reshape(D, NE * HE), s, _np.zeros((D, 32), w.dtype)], axis=1)
        return halves(w).reshape(128, 2, NC, 128).transpose(2, 0, 1, 3).reshape(NC, 128, 256)

    down = _np.concatenate([a["ffn_w_down"].reshape(NE * HE, D), a["ffn_sw_down"],
                            _np.zeros((32, D), a["ffn_w_down"].dtype)], axis=0).reshape(NC, 128, D)
    wf = _np.concatenate([chunked(a["ffn_w_gate"], a["ffn_sw_gate"]), chunked(a["ffn_w_up"], a["ffn_sw_up"]), down],
                         axis=2)

    def by_pairs(w):
        return halves(w).reshape(128, 2, 8, 2, 128).transpose(2, 0, 3, 1, 4).reshape(8, 128, 512)

    arrays = {
        "x_in": a["attn_x"].reshape(T, D),
        "ident_in": _np.eye(128, dtype=_np.float32),
        "less_in": _np.broadcast_to((_np.arange(NE)[None, :] < _np.arange(NE)[:, None]).astype(_np.float32).reshape(1, 64),
                                    (128, 64)),
        "gw_in": halves(a["ffn_gate_w"]).reshape(128, 2 * NE),
        "wf_in": wf,
        "wqi_in": by_pairs(a["attn_wq_idx"]),
        "ws_in": _np.concatenate([halves(a[k]).reshape(128, 256) for k in ("attn_wk_idx", "attn_wk", "attn_wv")], axis=1),
        "wiw_in": halves(a["attn_w_iw"]).reshape(128, 2 * NH),
        "wq_in": by_pairs(a["attn_wq"]),
        "wo_in": a["attn_wo"].reshape(8, 2, 128, D).transpose(0, 2, 1, 3).reshape(8, 128, 512),
    }
    nc = _bacc.Bacc("TRN2", target_bir_lowering=False, num_devices=1)
    args = []
    for name in arrays:
        arrays[name] = _np.ascontiguousarray(arrays[name])
        args.append(nc.dram_tensor(name, arrays[name].shape, _mybir.dt.from_np(arrays[name].dtype),
                                   kind="ExternalInput").ap())
    args.append(nc.dram_tensor("out_0", (T, D), _mybir.dt.float32, kind="ExternalOutput").ap())
    macaron_kernel(nc, *args)
    r = _run(nc, [arrays], core_ids=[0])
    return r.results[0]["out_0"].reshape(8, 256, D)
```

```python
import numpy as np
import concourse.bass as bass
import concourse.mybir as mybir
from contextlib import ExitStack

T = 2048
D = 256
NG = 4
GT = 512
NH = 16
NE = 8
HE = 176
NC = 14
ORDER = [11, 12, 13, 0, 1, 2, 3, 4, 5, 6, 7, 8, 9, 10]
NEG = -1e30
MARK = -3e38
SCALE = float(128) ** -0.5
EPS = 1e-5


def segments(c):
    out, at = [], 128 * c
    while at < 128 * (c + 1):
        e = at // HE
        end = min(128 * (c + 1), HE * (e + 1))
        out.append((at - 128 * c, end - at, e))
        at = end
    return out


def macaron_kernel(nc, x, ident_in, less_in, gw_in, wf_in, wqi_in, ws_in, wiw_in, wq_in, wo_in, out):
    f32 = mybir.dt.float32
    f32r = mybir.dt.float32r
    i32 = mybir.dt.int32
    ALU = mybir.AluOpType
    ACT = mybir.ActivationFunctionType
    AX = mybir.AxisListType

    ctx = ExitStack()
    with ctx:
        def sb(name, shape, dt=f32, stack=ctx):
            return stack.enter_context(nc.sbuf_tensor(name, shape, dt))

        X = sb("X", [128, 16, D])
        R1 = sb("R1", [128, 21504], f32r)
        R2 = sb("R2", [128, 9728], f32r)
        stage = sb("stage", [128, 2, 768])
        xf = sb("xf", [128, 2, GT])
        xh = sb("xh", [128, 2, 2, GT], f32r)
        xl = sb("xl", [128, 2, 2, GT], f32r)
        ident = sb("ident", [128, 128])
        gw = sb("gw", [128, 2, NE])
        wiw = sb("wiw", [128, 2, NH])
        st = sb("st", [128, 4, 6])
        mv = sb("mv", [128, 4, 2])
        nt = sb("nt", [128, 4, 4])
        PS = [ctx.enter_context(nc.psum_tensor(f"ps{i}", [128, 512], f32)) for i in range(8)]
        scratch = nc.dram_tensor("comb_scratch", [2 * NG, 32, 128], f32, kind="Internal").ap()

        prog = {e: [] for e in ("pe", "act", "dve", "pool", "sp")}
        count = {}
        last_of = {}

        def op(eng, fn, waits=(), sem=None):
            inc = 16 if eng == "sp" else 1
            if sem is None:
                sem = eng
            count[sem] = count.get(sem, 0) + inc
            last_of[eng] = (sem, count[sem])
            prog[eng].append((fn, list(waits), sem, inc))
            return (sem, count[sem])

        def quiet(eng, fn, waits=()):
            prog[eng].append((fn, list(waits), None, 0))

        def pe(sem, waits, mms):
            for n, (o, l, r, start, stop) in enumerate(mms):
                def fn(e, o=o, l=l, r=r, start=start, stop=stop):
                    return e.matmul(o, l, r, start=start, stop=stop, skip_group_check=True)
                w = waits if n == 0 else ()
                if n == len(mms) - 1:
                    return op("pe", fn, w, sem)
                quiet("pe", fn, w)

        def three(o, pairs, first=True, last=True):
            seq = [q for lh, ll, rh, rl in pairs for q in ((lh, rh), (lh, rl), (ll, rh))]
            return [(o, a, b, first and i == 0, last and i == len(seq) - 1) for i, (a, b) in enumerate(seq)]

        def f(ap):
            return ap.bitcast(f32)

        def copy(eng, o, i, waits, sem=None):
            if eng == "act":
                return op("act", lambda e: e.activation(o, i, ACT.Copy), waits, sem)
            return op(eng, lambda e: e.tensor_copy(o, i), waits, sem)

        def tt(eng, o, a, b, alu, waits, sem=None):
            return op(eng, lambda e: e.tensor_tensor(o, a, b, alu), waits, sem)

        def load(dst, src, waits, sem):
            return op("sp", lambda e: e.dma_start(dst, src), waits, sem)

        XT = [None] * NG
        XT[0] = load(X[:, 0:4, :], x[0:512, :].rearrange("(t p) d -> p t d", p=128), [], "x0")
        t_id = load(ident[:], ident_in, [], "c0")
        t_gw = load(gw[:], gw_in.rearrange("p (c e) -> p c e", c=2), [], "c1")

        stage_free = [[], []]
        nst = [0]

        def weight(src, n, dst, waits=(), eh="act", el="dve"):
            s = nst[0] % 2
            nst[0] += 1
            t = load(stage[:, s, 0:n], src, stage_free[s], f"w{s}")
            hi, lo = dst[:, 0:n], dst[:, n:2 * n]
            a = copy(eh, hi, stage[:, s, 0:n], [t, *waits], "split_" + eh)
            b = tt(el, lo, stage[:, s, 0:n], f(hi), ALU.subtract, [a], "split_" + el)
            stage_free[s] = [b]
            return b

        def rsqrt(v, w0):
            a, y, b = nt[:, :, 0], nt[:, :, 3], nt[:, :, 1]
            t = op("dve", lambda e: e.tensor_scalar(a, v, EPS, None, ALU.add), w0)
            t = op("dve", lambda e: e.tensor_scalar(b.bitcast(i32), a.bitcast(i32), 1, None,
                                                    ALU.logical_shift_right), [t])
            t = op("dve", lambda e: e.tensor_scalar(y.bitcast(i32), b.bitcast(i32), -1.0, float(0x5f3759df),
                                                    ALU.mult, ALU.add), [t])
            for _ in range(4):
                t = tt("dve", b, y, y, ALU.mult, [t])
                t = op("dve", lambda e: e.scalar_tensor_tensor(b, b, -0.5, a, ALU.mult, ALU.mult), [t])
                t = op("dve", lambda e: e.scalar_tensor_tensor(y, b, 1.5, y, ALU.add, ALU.mult), [t])
            return t

        def norm(g, ready, xn, xn_free):
            ts = []
            for i in range(4):
                t = op("dve", lambda e, i=i: e.bn_stats(st[:, i, :], X[:, 4 * g + i, :]), ready if i == 0 else [])
            for i in range(4):
                t = op("dve", lambda e, i=i: e.bn_aggr(mv[:, i, :], st[:, i, :]), [t] if i == 0 else [])
            t = rsqrt(mv[:, :, 1], [t])
            for i in range(4):
                t = op("dve", lambda e, i=i: e.tensor_scalar(xn[:, i, :], X[:, 4 * g + i, :], mv[:, i, 0:1],
                                                             nt[:, i, 3:4], ALU.subtract, ALU.mult),
                       [t] + xn_free if i == 0 else [], "xn")
            return t

        xbuf_free = [[], []]

        def flip(g, xn, t_xn, banks, bank_free):
            pts = []
            for dc in range(2):
                for i in range(4):
                    o, s = PS[banks[dc]][:, 128 * i:128 * i + 128], xn[:, i, 128 * dc:128 * dc + 128]
                    fn = lambda e, o=o, s=s: e.transpose(o, s, ident[:])
                    w = ([t_xn, t_id] if dc == 0 else []) + bank_free[dc] if i == 0 else []
                    if i == 3:
                        pts.append(op("pe", fn, w, "pe_xt"))
                    else:
                        quiet("pe", fn, w)
            b = g % 2
            for dc in range(2):
                ta = copy("act", xf[:, dc, :], PS[banks[dc]][:, :], [pts[1]], "xf")
            th = copy("dve", xh[:, b, :, :], xf[:, :, :], [ta] + xbuf_free[b], "xh")
            tl = tt("dve", xl[:, b, :, :], xf[:, :, :], f(xh[:, b, :, :]), ALU.subtract, [th], "xl")
            return ta, th, tl, pts[1]

        def ffn(n, res_ready, slots, wt, on_group, tail_loads, fetch, ahead, bank_free, ready0=None, hook=None):
            xn = xf[:, :, :].rearrange("p c (t d) -> p (c t) d", d=D)
            S = sb(f"S{n}", [128, 2, GT], f32, fs)
            TM = sb(f"TM{n}", [128, 2, GT], f32, fs)
            GH = sb(f"GH{n}", [128, 3, GT], f32r, fs)
            GL = sb(f"GL{n}", [128, 3, GT], f32r, fs)
            CB = sb(f"CB{n}", [128, 4, GT], f32, fs)
            LG = sb(f"LG{n}", [128, 4, NE], f32, fs)
            EX = sb(f"EX{n}", [128, 4, NE], f32, fs)
            G1 = sb(f"G1{n}", [128, 4, NE * NE], f32, fs)
            G2 = sb(f"G2{n}", [128, 4, NE * NE], f32, fs)
            less = sb(f"less{n}", [128, NE * NE], f32, fs)
            RK = sb(f"RK{n}", [128, 4, NE], f32, fs)
            mx = sb(f"mx{n}", [128, 4], f32, fs)
            sm = sb(f"sm{n}", [128, 4], f32, fs)
            CT = sb(f"CT{n}", [32, 128], f32, fs)
            t_less = load(less[:], less_in, tail_loads, "c2")
            free = {k: list(bank_free.get(k, [])) for k in range(8)}
            GB, UB, YB, RB = (0, 1), (2, 3), (4, 5), (6, 7)
            s_free, tm_free, cb_free = [[], []], [[], []], [[] for _ in range(4)]
            gh_free = [[], [], []]
            ncb = [0]
            XR = {}
            comb = {}
            lg_free, ct_free = [[]], [[]]

            nt_, rt = {}, {}

            def prep_norm(g):
                nt_[g] = norm(g, res_ready(g), xn, XR[g - 1][4] if g else [])

            def prep_flip(g):
                if g == 0 and ready0:
                    XR[g] = ready0
                else:
                    XR[g] = flip(g, xn, nt_[g], RB, [free[6], free[7]])
                free[6] = free[7] = free[7] + [XR[g][0]]

            def prep_route(g):
                ta, th, tl, tp = XR[g]
                mms = [(PS[6][:, NE * i:NE * i + NE], xf[:, dc, 128 * i:128 * i + 128], gw[:, dc, :], dc == 0, dc == 1)
                       for i in range(4) for dc in range(2)]
                tg = pe("pe_gate", [ta, t_gw] + free[6], mms)
                XR[g] = (ta, th, tl, tp, [tg, tl])
                lg = PS[6][:, 0:32].rearrange("p (t e) -> p t e", e=NE)
                t = copy("dve", LG[:], lg, [tg] + lg_free[0])
                free[6] = [t]
                t = op("dve", lambda e: e.tensor_reduce(mx[:], LG[:], AX.X, ALU.max), [t])
                bc = lambda a: a[:, :].rearrange("p (t o) -> p t o", o=1).to_broadcast([128, 4, NE])
                t = tt("dve", EX[:], LG[:], bc(mx), ALU.subtract, [t])
                te = op("act", lambda e: e.activation(EX[:], EX[:], ACT.Exp), [t])
                four = [128, 4, NE, NE]
                j_ = LG[:, :, :].rearrange("p t (o e) -> p t o e", o=1).to_broadcast(four)
                e_ = LG[:, :, :].rearrange("p t (e o) -> p t e o", o=1).to_broadcast(four)
                g4 = lambda a: a[:, :, :].rearrange("p t (e j) -> p t e j", j=NE)
                for q in range(4):
                    jq = LG[:, q, :].rearrange("p (o e) -> p o e", o=1).to_broadcast([128, NE, NE])
                    eq = LG[:, q, :].rearrange("p (e o) -> p e o", o=1).to_broadcast([128, NE, NE])
                    gq = lambda a: a[:, q, :].rearrange("p (e j) -> p e j", j=NE)
                    t1 = tt("dve", gq(G1), jq, eq, ALU.is_gt, [])
                    t2 = tt("dve", gq(G2), jq, eq, ALU.is_ge, [])
                lb = less[:, :].rearrange("p (o n) -> p o n", o=1).to_broadcast([128, 4, NE * NE])
                t2 = tt("dve", G2[:], G2[:], lb, ALU.mult, [t2, t_less])
                t2 = tt("dve", G1[:], G1[:], G2[:], ALU.max, [t2])
                t2 = op("dve", lambda e: e.tensor_reduce(RK[:], g4(G1), AX.X, ALU.add), [t2])
                t = op("dve", lambda e: e.tensor_reduce(sm[:], EX[:], AX.X, ALU.add), [te])
                t = op("dve", lambda e: e.reciprocal(sm[:], sm[:]), [t])
                t = tt("dve", EX[:], EX[:], bc(sm), ALU.mult, [t])
                t = op("dve", lambda e: e.scalar_tensor_tensor(EX[:], RK[:], 2.0, EX[:], ALU.is_lt, ALU.mult), [t])
                lg_free[0] = [t]
                rt[g] = t

            def prep_comb(g):
                t = pe("pe_gate", [rt[g], t_id] + free[7],
                       [(PS[7][0:32, 0:128], EX[:, :, :].rearrange("p t e -> p (t e)"), ident[:], True, True)])
                t = copy("act", CT[:], PS[7][0:32, 0:128], [t] + ct_free[0])
                free[7] = [t]
                comb[g] = load(scratch[NG * n + g], CT[:], [t], f"cs{g % 2}")
                ct_free[0] = [comb[g]]

            def combine_rows(g, c):
                k = ncb[0] % 4
                ncb[0] += 1
                for i, (p, rows, e) in enumerate(segments(c)):
                    src = scratch[NG * n + g].rearrange("(t e) q -> e t q", e=NE)[e:e + 1, :, :]
                    t = load(CB[p:p + rows, k, :].rearrange("p (t q) -> p t q", q=128),
                             src.to_broadcast([rows, 4, 128]), [comb[g]] + cb_free[k], f"cb{k}")
                return k, t

            for i in range(ahead):
                fetch(i)
            if not ready0:
                prep_norm(0)
            prep_flip(0)
            prep_route(0)
            tasks = [(g, i) for g in range(NG) for i in range(NC)]
            cbs = {}
            routed = [(g, i) for g, i in tasks if ORDER[i] < 11]
            down_q = {}

            def down(g, i, tok, k3):
                c = ORDER[i]
                w = slots[c]
                for a in range(4):
                    y = PS[YB[a // 2]][:, 256 * (a % 2):256 * (a % 2) + 256]
                    sl = slice(128 * a, 128 * a + 128)
                    mms = [(y, GH[:, k3, sl], w[:, 512:768]), (y, GH[:, k3, sl], w[:, 1280:1536]),
                           (y, GL[:, k3, sl], w[:, 512:768])]
                    mms = [(*m, i == 0 and a % 2 == 0 and q == 0, i == NC - 1 and q == 2) for q, m in enumerate(mms)]
                    wts = [*tok] if a == 0 else []
                    if i == 0:
                        wts = wts + free[YB[a // 2]]
                    t = pe("pe_down", wts, mms)
                gh_free[k3] = [t]
                if i == NC - 1:
                    for b in range(2):
                        xs = X[:, 4 * g + 2 * b:4 * g + 2 * b + 2, :]
                        y = PS[YB[b]][:, :].rearrange("p (t d) -> p t d", d=D)
                        tx = op("dve", lambda e, xs=xs, y=y: e.scalar_tensor_tensor(xs, y, 0.5, xs, ALU.mult, ALU.add),
                                [t], "xres")
                        free[YB[b]] = [tx]
                    on_group(g, tx)
                return t

            last = None
            for s, (g, i) in enumerate(tasks + [None, None]) if False else enumerate(tasks + [(None, None)] * 2):
                if g is not None:
                    c = ORDER[i]
                    w = slots[c]
                    if g == 0 and i + ahead < NC:
                        fetch(i + ahead)
                    if i == 0 and g > 0:
                        for r in range(4):
                            cbs[(g, 3 + r)] = combine_rows(g, ORDER[3 + r])
                    ta, th, tl, tp, _ = XR[g]
                    b = g % 2
                    toks = []
                    for z, banks in enumerate((GB, UB)):
                        bk = banks[s % 2]
                        pairs = [(w[:, z * 256 + dc * 128:z * 256 + dc * 128 + 128],
                                  w[:, 768 + z * 256 + dc * 128:768 + z * 256 + dc * 128 + 128],
                                  xh[:, b, dc, :], xl[:, b, dc, :]) for dc in range(2)]
                        toks.append(pe("pe_gu", [th, tl, wt[c]] + free[bk], three(PS[bk][:, :], pairs)))
                    if i == NC - 1:
                        xbuf_free[b] = [toks[1]]
                    k2, k3 = s % 2, s % 3
                    t = op("act", lambda e, k2=k2, gb=GB[s % 2]: e.activation(S[:, k2, :], PS[gb][:, :], ACT.Silu),
                           [toks[0]] + s_free[k2], "silu")
                    free[GB[s % 2]] = [t]
                    t = tt("dve", TM[:, k2, :], S[:, k2, :], PS[UB[s % 2]][:, :], ALU.mult, [t, toks[1]] + tm_free[k2])
                    free[UB[s % 2]] = [t]
                    s_free[k2] = [t]
                    if c < 11:
                        k4, tc = cbs.pop((g, i))
                        t = tt("dve", TM[:, k2, :], TM[:, k2, :], CB[:, k4, :], ALU.mult, [t, tc])
                        cb_free[k4] = [t]
                        if i + 4 < NC:
                            cbs[(g, i + 4)] = combine_rows(g, ORDER[i + 4])
                    t1 = copy("act", GH[:, k3, :], TM[:, k2, :], [t] + gh_free[k3], "gh")
                    t2 = tt("dve", GL[:, k3, :], TM[:, k2, :], f(GH[:, k3, :]), ALU.subtract, [t1, *gh_free[k3]], "gl")
                    tm_free[k2] = [t2]
                    down_q[s] = (g, i, (t1, t2), k3)
                if s - 2 in down_q:
                    last = down(*down_q.pop(s - 2))
                if g == 0 and i == 0:
                    prep_comb(0)
                    for r in range(4):
                        cbs[(g, 3 + r)] = combine_rows(g, ORDER[3 + r])
                if g is not None and g + 1 < NG:
                    if i == 3:
                        prep_norm(g + 1)
                    elif i == 5:
                        prep_flip(g + 1)
                    elif i == 6:
                        prep_route(g + 1)
                    elif i == 10:
                        prep_comb(g + 1)
                if g == NG - 1 and hook:
                    hook(i, free, XR[g][4])
            return free, [last]

        fs = ExitStack()
        slots1 = {c: R1[:, 1536 * c:1536 * c + 1536] for c in range(NC)}
        wt1 = {}

        def fetch1(n):
            c = ORDER[n]
            wt1[c] = weight(wf_in[c], 768, slots1[c])
            if n == 2:
                for g in range(1, NG):
                    XT[g] = load(X[:, 4 * g:4 * g + 4, :],
                                 x[512 * g:512 * g + 512, :].rearrange("(t p) d -> p t d", p=128), [], f"x{g}")

        late = {}

        def after_group1(g, t):
            xres[g] = t
            if g == 0:
                late["iw"] = load(wiw[:], wiw_in.rearrange("p (c e) -> p c e", c=2), [], "c3")
                late["small"] = weight(ws_in, 768, R2[:, 8192:9728], (), "pool", "pool")
                late["wqi"] = [weight(wqi_in[k], 512, R2[:, 1024 * k:1024 * k + 1024], (), "pool", "pool")
                               for k in range(8)]

        xres = [None] * NG

        xn = xf[:, :, :].rearrange("p c (t d) -> p (c t) d", d=D)
        XR, normed = {}, {}

        def into_attention(i, free, xn_free):
            if i == 4:
                normed[0] = norm(0, [xres[0]], xn, xn_free)
            if i == 7:
                XR[0] = flip(0, xn, normed[0], (6, 7), [free[6], free[7]])
                free[6] = free[7] = [XR[0][0]]

        free1, last1 = ffn(0, lambda g: [XT[g]], slots1, wt1, after_group1, [], fetch1, 3, {}, None, into_attention)
        t_iw, t_small, t_wqi = late["iw"], late["small"], late["wqi"]
        fs.close()
        edge = [last_of[e] for e in ("pe", "act", "dve")]

        fs = ExitStack()
        A = lambda name, shape, dt=f32: sb(name, shape, dt, fs)
        PTH = R1[:, 16384:17152].rearrange("p (h n) -> p h n", h=2)
        PTL = R1[:, 17152:17920].rearrange("p (h n) -> p h n", h=2)
        OH, OL = R1[:, 17920:18432], R1[:, 18432:18944]
        QIH = R1[:, 18944:19200].rearrange("p (b n) -> p b n", b=2)
        QIL = R1[:, 19200:19456].rearrange("p (b n) -> p b n", b=2)
        QH = R1[:, 19456:20480].rearrange("p (r b n) -> p r b n", r=4, b=2)
        QL = R1[:, 20480:21504].rearrange("p (r b n) -> p r b n", r=4, b=2)
        QF = A("QF", [128, 4, 2, 128])
        KF = A("KF", [128, 2, 128])
        KH, KL = A("KH", [128, GT], f32r), A("KL", [128, GT], f32r)
        VH, VL = A("VH", [128, 4, 128], f32r), A("VL", [128, 4, 128], f32r)
        SP = A("SP", [128, 2, 2, 384])
        IM = A("IM", [128, 768])
        W = A("W", [128, 2, 768])
        M8 = A("M8", [128, 4, 8])
        MX = A("MX", [128, 2, 4])
        NB = A("NB", [128, 2, 4])
        SM = A("SM", [128, 2, 4])
        RC = A("RC", [128, 2, 4])
        KIF = A("KIF", [128, 2, 128])
        KIH, KIL = A("KIH", [128, GT], f32r), A("KIL", [128, GT], f32r)
        R = A("R", [128, 2, 384])
        I = A("I", [128, 768])
        IW = A("IW", [128, 4, NH])
        QIF = A("QIF", [128, 2, 128])
        QB, SB_, TB, OB, YB = 0, (1, 2), (3, 4), 5, (6, 7)
        free = {k: list(v) for k, v in free1.items()}
        t_wq = [weight(wq_in[k], 512, R1[:, 1024 * k:1024 * k + 1024], edge, "pool", "pool") for k in range(8)]
        t_wo = [weight(wo_in[k], 512, R1[:, 8192 + 1024 * k:8192 + 1024 * k + 1024], edge, "pool", "pool") for k in range(8)]
        xn_free = [[]]
        rf = {k: list(edge) for k in ("k", "w0", "w1", "im0", "im1", "im2", "im3", "o", "pt", "v", "sp0", "sp1",
                                      "q0", "q1", "q2", "q3", "qi", "ki", "iw", "r0", "r1")}
        rf |= {k: [] for k in ("i0", "i1", "i2", "i3")}
        TILES = [(b, h, 384 * b + 128 * h, 128 * (h + 1)) for b in range(2) for h in range(2)]

        def do_norm(g):
            normed[g] = norm(g, [xres[g]], xn, xn_free[0])

        def small(kind, hl, dc):
            o = 8192 + 768 * hl + 256 * kind + 128 * dc
            return R2[:, o:o + 128]

        tk = {}

        def project(kind, g):
            b = g % 2
            _, th, tl, _ = XR[g]
            pairs = [(small(kind, 0, dc), small(kind, 1, dc), xh[:, b, dc, :], xl[:, b, dc, :]) for dc in range(2)]
            t = pe("pe_k", [th, tl, t_small] + free[QB], three(PS[QB][:, :], pairs))
            KX_F, KX_H, KX_L, name = ((KIF, KIH, KIL, "ki"), (KF, KH, KL, "k"))[kind]
            p2 = PS[QB][:, :].rearrange("p (b n) -> p b n", b=2)
            t1 = copy("act", KX_F[:, :, :], p2[:, :, 0:128], [t] + rf[name])
            t2 = copy("act", KX_H[:, :], PS[QB][:, :], rf[name], "kh")
            t3 = tt("dve", KX_L[:, :], PS[QB][:, :], f(KX_H[:, :]), ALU.subtract, [t2] + rf[name], "kl")
            free[QB] = [t3]
            tk[name] = [t1, t2, t3]

        def values(g):
            b = g % 2
            _, th, tl, _ = XR[g]
            ts = []
            for a in range(4):
                bk = TB[a // 2]
                o = PS[bk][:, 256 * (a % 2):256 * (a % 2) + 256]
                seq = []
                for dc in range(2):
                    wv = R2[:, 8192:9728].rearrange("p (l n) -> p l n", l=2)[:, :, 512 + 128 * dc:640 + 128 * dc]
                    for s_ in (xh, xl):
                        seq.append((s_[:, b, dc, 128 * a:128 * a + 128], wv))
                mms = [(o, l, r, n == 0, n == 3) for n, (l, r) in enumerate(seq)]
                ts.append(pe("pe_v", free[bk] if a % 2 == 0 else [], mms))
            for z in range(2):
                src = PS[TB[z]][:, :].rearrange("p (t l n) -> p t l n", t=2, l=2)
                t1 = copy("act", R[:, 0, 0:256].rearrange("p (t n) -> p t n", t=2),
                          src[:, :, 1, :], [ts[2 * z + 1]] + rf["r0"])
                rv = R[:, 0, 0:256].rearrange("p (t n) -> p t n", t=2)
                t2 = tt("dve", rv, rv, src[:, :, 0, :], ALU.add, [t1])
                free[TB[z]] = [t2]
                t3 = copy("dve", VH[:, 2 * z:2 * z + 2, :], rv, [t2] + rf["v"], "vh")
                t4 = tt("dve", VL[:, 2 * z:2 * z + 2, :], rv, f(VH[:, 2 * z:2 * z + 2, :]), ALU.subtract,
                        [t3], "vl")
                rf["r0"] = [t4]
            tk["v"] = [t3, t4]

        def weights_of_heads(g):
            ta = XR[g][0]
            mms = [(PS[SB_[0]][:, NH * i:NH * i + NH], xf[:, dc, 128 * i:128 * i + 128], wiw[:, dc, :], dc == 0, dc == 1)
                   for i in range(4) for dc in range(2)]
            t = pe("pe_iw", [ta, t_iw] + free[SB_[0]], mms)
            xn_free[0] = [t, XR[g][2]]
            t = copy("dve", IW[:], PS[SB_[0]][:, 0:64].rearrange("p (t e) -> p t e", e=NH), [t] + rf["iw"])
            free[SB_[0]] = [t]
            tk["iw"] = [t]

        def flip_group(g):
            XR[g] = flip(g, xn, normed[g], SB_, [free[SB_[0]], free[SB_[1]]])
            free[SB_[0]] = free[SB_[1]] = [XR[g][0]]

        bias = {}

        def topk(g):
            pieces = []
            for i, (b, h, o, n) in enumerate(TILES):
                Is, Ms, Ws = I[:, o:o + n], IM[:, o:o + n], W[:, g % 2, o:o + n]
                tok = {}

                def causal(Is=Is, Ms=Ms, n=n, h=h, i=i, tok=tok):
                    tok[0] = op("pool", lambda e: e.affine_select(
                        out=Ms, in_=Is, compare_op=ALU.is_ge, fill=NEG, base=128 * h, pattern=[[-1, n]],
                        channel_multiplier=1), [tk[f"i{i}"]] + rf[f"im{i}"])
                    rf[f"i{i}"] = [tok[0]]

                def best(src, Ws=Ws, i=i, tok=tok):
                    t = op("dve", lambda e: e.max(M8[:, i, :], src), [tok[0]])
                    tok[0] = op("dve", lambda e: e.match_replace(Ws, M8[:, i, :], src, MARK), [t] + rf[f"w{g % 2}"])

                def mask(Ms=Ms, Ws=Ws, i=i, tok=tok):
                    t = op("dve", lambda e: e.tensor_scalar(Ws, Ws, MARK, None, ALU.not_equal), [tok[0]])
                    t = op("dve", lambda e: e.scalar_tensor_tensor(Ws, Ms, NEG / 2, Ws, ALU.is_le, ALU.max), [t])
                    rf[f"im{i}"] = [t]
                    bias[(g, i)] = op("dve", lambda e: e.tensor_scalar(Ws, Ws, NEG, None, ALU.mult), [t])

                pieces.append(causal)
                for r in range(4):
                    pieces.append(lambda best=best, src=Ms if r == 0 else Ws: best(src))
                pieces.append(mask)
            return [p for n, p in enumerate(pieces) if n % 6 == 0] + [p for n, p in enumerate(pieces) if n % 6]

        def head(g, h, wsrc, wtok, F, H, L, wf_, sem, bank=QB):
            b = g % 2
            _, th, tl, _ = XR[g]
            k, i = h // 2, h % 2
            w = wsrc[:, 1024 * k:1024 * k + 1024]
            pairs = [(w[:, 256 * i + 128 * dc:256 * i + 128 * dc + 128],
                      w[:, 512 + 256 * i + 128 * dc:512 + 256 * i + 128 * dc + 128],
                      xh[:, b, dc, :], xl[:, b, dc, :]) for dc in range(2)]
            t = pe(sem, [th, tl, wtok[k]] + free[bank], three(PS[bank][:, :], pairs))
            p2 = PS[bank][:, :].rearrange("p (b z n) -> p b z n", b=2, z=2)
            t1 = copy("act", F, p2[:, :, 0, :], [t] + rf[wf_], sem + "f")
            t2 = copy("act", H, p2[:, :, 1, :], rf[wf_], sem + "h")
            t3 = tt("dve", L, p2[:, :, 1, :], f(H), ALU.subtract, [t2] + rf[wf_], sem + "l")
            free[bank] = [t3]
            if h == NH - 1 and sem == "pe_q":
                xbuf_free[b] = [t]
            return [t1, t2, t3]

        def products(bank, b, F, H, L, KXF, KXH, KXL, waits, sem):
            o = PS[bank]
            kb = slice(256 * b, 256 * b + 256)
            mms = [(o[:, 0:128], F[:, b, :], KXF[:, b, :], True, True)]
            mms += three(o[:, 128:384], [(H[:, b, :], L[:, b, :], KXH[:, kb], KXL[:, kb])])
            return pe(sem, waits + free[bank], mms)

        def qi_of(g, h):
            if g == 0:
                r = h % 4
                return QF[:, r, :, :], QH[:, r, :, :], QL[:, r, :, :], f"q{r}"
            return QIF, QIH, QIL, "qi"

        def idx_project(g, h):
            F, H, L, name = qi_of(g, h)
            tk[f"qi{h}"] = head(g, h, R2, t_wqi, F[:, :, :], H[:, :, :], L[:, :, :], name, "pe_qi",
                                (QB, OB)[h % 2] if g == 0 else QB)

        def idx_logits(g, h):
            F, H, L, name = qi_of(g, h)
            for b in range(2):
                t = products(SB_[b], b, F, H, L, KIF, KIH, KIL, tk[f"qi{h}"] + tk["ki"], "pe_l")
                tr = op("act", lambda e, b=b: e.activation(R[:, b, :], PS[SB_[b]][:, 0:384], ACT.Relu),
                        [t] + rf[f"r{b}"], "relu")
                free[SB_[b]] = [tr]
                for z in range(2):
                    i = 2 * b + z
                    o, n = 384 * b + 128 * z, 128 * (z + 1)
                    r, Is, iw = R[:, b, 128 * z:128 * z + n], I[:, o:o + n], IW[:, i, h:h + 1]
                    if h == 0:
                        ta = op("dve", lambda e, r=r, Is=Is, iw=iw: e.tensor_scalar(Is, r, iw, None, ALU.mult),
                                [tr, *tk["iw"]] + rf[f"i{i}"], "acc")
                    else:
                        ta = op("dve", lambda e, r=r, Is=Is, iw=iw: e.scalar_tensor_tensor(
                            Is, r, iw, Is, ALU.mult, ALU.add), [tr, tk[f"i{i}"]], "acc")
                    tk[f"i{i}"] = ta
                rf[f"r{b}"] = [ta]
            rf[name] = [t]
            if h == NH - 1:
                rf["ki"] = [t]
                rf["iw"] = [ta]

        qt = {}
        SMT, PTT, OT, YT = {}, {}, {}, {}

        def main_project(U):
            g, u = divmod(U, 16)
            r = u % 4
            qt[U] = head(g, u, R1, t_wq, QF[:, r, :, :], QH[:, r, :, :], QL[:, r, :, :], f"q{r}", "pe_q")

        def scores(U):
            g, u = divmod(U, 16)
            j, b = divmod(u, 2)
            k = U % 2
            for i in range(2):
                h = 2 * j + i
                r = h % 4
                t = products(SB_[i], b, QF[:, r, :, :], QH[:, r, :, :], QL[:, r, :, :], KF, KH, KL,
                             qt[16 * g + h] + tk["k"], "pe_s")
                if b == 1:
                    rf[f"q{r}"] = [t]
                for z in range(2):
                    n, o = 128 * (z + 1), 128 * z
                    tm = op("dve", lambda e, i=i, z=z, n=n, o=o, k=k, b=b, g=g: e.tensor_tensor_reduce(
                        out=SP[:, k, i, o:o + n], in0=PS[SB_[i]][:, o:o + n], in1=W[:, g % 2, 384 * b + o:384 * b + o + n],
                        scale=1.0, scalar=-3e38, op0=ALU.add, op1=ALU.max, accum_out=MX[:, k, 2 * i + z:2 * i + z + 1]),
                        [t, bias[(g, 2 * b + z)]] + rf[f"sp{k}"], "mask")
                free[SB_[i]] = [tm]
            tn = op("dve", lambda e, k=k: e.tensor_scalar(NB[:, k, :], MX[:, k, :], -SCALE, None, ALU.mult), [tm], "nb")
            for i in range(2):
                for z in range(2):
                    n, o = 128 * (z + 1), 128 * z
                    te = op("act", lambda e, i=i, z=z, n=n, o=o, k=k: e.activation(
                        SP[:, k, i, o:o + n], SP[:, k, i, o:o + n], ACT.Exp, scale=SCALE,
                        bias=NB[:, k, 2 * i + z:2 * i + z + 1], accum_out=SM[:, k, 2 * i + z:2 * i + z + 1]),
                        [tn], "exp")
            SMT[U] = te
            if u == 15:
                rf["k"] = [t]
                rf[f"w{g % 2}"] = [tm]

        def normalise(U):
            k = U % 2
            t = op("dve", lambda e, k=k: e.reciprocal(RC[:, k, :], SM[:, k, :]), [SMT[U]], "rc")
            for i in range(2):
                for z in range(2):
                    n, o = 128 * (z + 1), 128 * z
                    t = op("dve", lambda e, i=i, z=z, n=n, o=o, k=k: e.tensor_scalar(
                        SP[:, k, i, o:o + n], SP[:, k, i, o:o + n], RC[:, k, 2 * i + z:2 * i + z + 1], None, ALU.mult),
                        [t], "pn")
            SMT[U] = t

        def flip_p(U):
            k = U % 2
            for i in range(2):
                o = PS[TB[i]]
                srcs = [SP[:, k, i, 0:128], SP[:, k, i, 128:256], SP[:, k, i, 256:384]]
                for z, s_ in enumerate(srcs):
                    fn = lambda e, o=o, z=z, s_=s_: e.transpose(o[:, 128 * z:128 * z + 128], s_, ident[:])
                    w = [SMT[U]] + free[TB[i]] if z == 0 else []
                    if z == 2:
                        t = op("pe", fn, w, "pe_t")
                    else:
                        quiet("pe", fn, w)
                th = copy("act", PTH[:, i, :], o[:, 0:384], [t] + rf["pt"], "pth")
                tl = tt("dve", PTL[:, i, :], o[:, 0:384], f(PTH[:, i, :]), ALU.subtract, [th] + rf["pt"], "ptl")
                free[TB[i]] = [tl]
            rf[f"sp{k}"] = [t]
            PTT[U] = [th, tl]

        def pv(U):
            g, u = divmod(U, 16)
            b = u % 2
            o = PS[OB]
            o2 = o[:, :].rearrange("p (h n) -> p h n", h=2)
            mms = []
            mms += three(o2[:, :, :], [(VH[:, 2 * b, :], VL[:, 2 * b, :], PTH[:, :, 0:256], PTL[:, :, 0:256])],
                         True, False)
            mms += three(o2[:, :, 128:256], [(VH[:, 2 * b + 1, :], VL[:, 2 * b + 1, :],
                                              PTH[:, :, 256:384], PTL[:, :, 256:384])], False, True)
            t = pe("pe_o", PTT[U] + tk[f"v_{g}"] + free[OB], mms)
            rf["pt"] = [t]
            if u == 15:
                rf["v"] = [t]
            th = copy("dve", OH, o[:, :], [t] + rf["o"], "oh")
            tl = tt("dve", OL, o[:, :], f(OH), ALU.subtract, [th], "ol")
            free[OB] = [tl]
            OT[U] = [th, tl]

        outs = []

        def wo(U):
            g, u = divmod(U, 16)
            j, b = divmod(u, 2)
            bank = YB[b]
            first = True
            for i in range(2):
                h = 2 * j + i
                w = R1[:, 8192 + 1024 * (h // 2):8192 + 1024 * (h // 2) + 1024]
                wh, wl = w[:, 256 * (h % 2):256 * (h % 2) + 256], w[:, 512 + 256 * (h % 2):512 + 256 * (h % 2) + 256]
                for z in range(2):
                    sl = slice(256 * i + 128 * z, 256 * i + 128 * z + 128)
                    y = PS[bank][:, 256 * z:256 * z + 256]
                    mms = [(y, OH[:, sl], wh), (y, OH[:, sl], wl), (y, OL[:, sl], wh)]
                    mms = [(*m, j == 0 and i == 0 and z == 0 and q == 0, j == 7 and i == 1 and q == 2)
                           for q, m in enumerate(mms)]
                    wts = OT[U] + [t_wo[h // 2]] if i == 0 and z == 0 else []
                    if j == 0 and first:
                        wts = wts + free[bank]
                    first = False
                    t = pe("pe_y", wts, mms)
            rf["o"] = [t]
            if j == 7:
                xs = X[:, 4 * g + 2 * b:4 * g + 2 * b + 2, :]
                y = PS[bank][:, :].rearrange("p (t d) -> p t d", d=D)
                tx = tt("dve", xs, xs, y, ALU.add, [t], "xres")
                free[bank] = [tx]
                xres[g] = tx

        slots2, wt2 = {}, {}
        for n, c in enumerate(ORDER):
            slots2[c] = R2[:, 1536 * n:1536 * n + 1536] if n < 6 else R1[:, 1536 * (n - 6):1536 * (n - 6) + 1536]

        def fetch2(n):
            if n >= 6:
                wt2[ORDER[n]] = weight(wf_in[ORDER[n]], 768, slots2[ORDER[n]], edge2)

        project(0, 0)
        weights_of_heads(0)
        do_norm(1)
        idx_project(0, 0)
        for h in range(NH):
            if h + 1 < NH:
                idx_project(0, h + 1)
            idx_logits(0, h)
            if h == 8:
                flip_group(1)
        pend = topk(0)

        def drip(n):
            for _ in range(min(n, len(pend))):
                pend.pop(0)()

        def begin_idx(g):
            project(0, g)
            weights_of_heads(g)

        drip(8)
        begin_idx(1)
        drip(4)
        idx_project(1, 0)
        main_project(0)
        drip(4)
        idx_logits(1, 0)
        main_project(1)
        idx_project(1, 1)
        drip(8)
        idx_logits(1, 1)
        for U in range(64):
            g, u = divmod(U, 16)
            V = U + 18
            gi, hi = divmod(V, 16)
            idx = gi < NG
            if u == 0:
                project(1, g)
            if u > 0 and idx:
                idx_project(gi, hi)
            if u > 0:
                scores(U)
            drip(4)
            if U >= 3:
                wo(U - 3)
            if U >= 2:
                pv(U - 2)
            if u == 1:
                values(g)
                tk[f"v_{g}"] = tk["v"]
            if U >= 1:
                flip_p(U - 1)
            drip(4)
            if u == 0 and idx:
                idx_project(gi, hi)
            if u == 0:
                scores(U)
            if U + 2 < 64:
                main_project(U + 2)
            if idx:
                idx_logits(gi, hi)
            drip(4)
            normalise(U)
            if u == 9 and g + 2 < NG:
                do_norm(g + 2)
            if u == 13:
                if g + 1 < NG:
                    pend = topk(g + 1)
                    for _ in range(4):
                        pend.pop(0)()
                if g + 2 < NG:
                    flip_group(g + 2)
                    begin_idx(g + 2)
                if g == NG - 2:
                    r2_edge = [(s, count[s]) for s in ("pe_qi", "pe_k", "pe_v")]
            if g == NG - 1:
                if u % 2 == 1 and u < 12:
                    n = u // 2
                    wt2[ORDER[n]] = weight(wf_in[ORDER[n]], 768, slots2[ORDER[n]],
                                           [*r2_edge, ("pe_k", count["pe_k"]), ("pe_v", count["pe_v"])])
                if u == 6:
                    t2n = norm(0, [xres[0]], xn, xn_free[0])
                if u == 10:
                    ready2 = flip(0, xn, t2n, SB_, [free[SB_[0]], free[SB_[1]]])
                    free[SB_[0]] = free[SB_[1]] = [ready2[0]]
        for U in (64, 65, 66):
            wo(U - 3)
            if U < 66:
                pv(U - 2)
            if U < 65:
                flip_p(U - 1)
        fs.close()
        edge2 = [last_of[e] for e in ("pe", "act", "dve")]

        fs = ExitStack()

        def store(g, t):
            outs.append(load(out[512 * g:512 * g + 512, :].rearrange("(t p) d -> p t d", p=128),
                             X[:, 4 * g:4 * g + 4, :], [t], f"out{g}"))

        ffn(1, lambda g: [xres[g], *edge2], slots2, wt2, store, edge2, fetch2, 6, {k: edge2 for k in range(8)}, ready2)
        fs.close()

        sems = {s: ctx.enter_context(nc.semaphore(f"s_{s}")) for s in count}
        block = ctx.enter_context(nc.Block())

        def run(e, name):
            seen = {}
            for fn, waits, sem, inc in prog[name]:
                for s, v in waits:
                    if seen.get(s, 0) < v:
                        e.wait_ge(sems[s], v)
                        seen[s] = v
                ins = fn(e)
                if sem is not None:
                    ins.then_inc(sems[sem], inc)

        @block.tensor
        def _(e):
            run(e, "pe")

        @block.scalar
        def _(e):
            run(e, "act")

        @block.vector
        def _(e):
            run(e, "dve")

        @block.gpsimd
        def _(e):
            run(e, "pool")

        @block.sync
        def _(e):
            run(e, "sp")
            for s, v in outs:
                e.wait_ge(sems[s], v)


def kernel(**inputs):
    import numpy as _np
    import concourse.bacc as _bacc
    from concourse import mybir as _mybir
    from concourse.bass_utils import run_bass_kernel_spmd as _run

    a = {k[3:]: _np.asarray(v) for k, v in inputs.items()}

    def halves(w):
        return w.reshape(2, 128, w.shape[1]).transpose(1, 0, 2)

    def chunked(w, s):
        w = _np.concatenate([w.transpose(1, 0, 2).reshape(D, NE * HE), s, _np.zeros((D, 32), w.dtype)], axis=1)
        return halves(w).reshape(128, 2, NC, 128).transpose(2, 0, 1, 3).reshape(NC, 128, 256)

    down = _np.concatenate([a["ffn_w_down"].reshape(NE * HE, D), a["ffn_sw_down"],
                            _np.zeros((32, D), a["ffn_w_down"].dtype)], axis=0).reshape(NC, 128, D)
    wf = _np.concatenate([chunked(a["ffn_w_gate"], a["ffn_sw_gate"]), chunked(a["ffn_w_up"], a["ffn_sw_up"]), down],
                         axis=2)

    def by_pairs(w):
        return halves(w).reshape(128, 2, 8, 2, 128).transpose(2, 0, 3, 1, 4).reshape(8, 128, 512)

    arrays = {
        "x_in": a["attn_x"].reshape(T, D),
        "ident_in": _np.eye(128, dtype=_np.float32),
        "less_in": _np.broadcast_to((_np.arange(NE)[None, :] < _np.arange(NE)[:, None]).astype(_np.float32).reshape(1, 64),
                                    (128, 64)),
        "gw_in": halves(a["ffn_gate_w"]).reshape(128, 2 * NE),
        "wf_in": wf,
        "wqi_in": by_pairs(a["attn_wq_idx"]),
        "ws_in": _np.concatenate([halves(a[k]).reshape(128, 256) for k in ("attn_wk_idx", "attn_wk", "attn_wv")], axis=1),
        "wiw_in": halves(a["attn_w_iw"]).reshape(128, 2 * NH),
        "wq_in": by_pairs(a["attn_wq"]),
        "wo_in": a["attn_wo"].reshape(8, 2, 128, D).transpose(0, 2, 1, 3).reshape(8, 128, 512),
    }
    nc = _bacc.Bacc("TRN2", target_bir_lowering=False, num_devices=1)
    args = []
    for name in arrays:
        arrays[name] = _np.ascontiguousarray(arrays[name])
        args.append(nc.dram_tensor(name, arrays[name].shape, _mybir.dt.from_np(arrays[name].dtype),
                                   kind="ExternalInput").ap())
    args.append(nc.dram_tensor("out_0", (T, D), _mybir.dt.float32, kind="ExternalOutput").ap())
    macaron_kernel(nc, *args)
    r = _run(nc, [arrays], core_ids=[0])
    return r.results[0]["out_0"].reshape(8, 256, D)
```

```python
import numpy as np
import concourse.bass as bass
import concourse.mybir as mybir
from contextlib import ExitStack

T = 2048
D = 256
NG = 4
GT = 512
NH = 16
NE = 8
HE = 176
NT = 23
BLOCK = 2432
PLACES = ([4608 + BLOCK * e for e in range(8)],
          [21504 + 4608, 21504 + 7040, 0, 2432, 4864, 8192, 10624, 13056])
NEG = -1e30
MARK = -3e38
SCALE = float(128) ** -0.5
EPS = 1e-5


def macaron_kernel(nc, x, cst_in, row_in, tok_in, gw_in, wsh_in, wex_in, wqi_in, ws_in, wiw_in, wq_in, wo_in, out):
    f32 = mybir.dt.float32
    f32r = mybir.dt.float32r
    i32 = mybir.dt.int32
    u32 = mybir.dt.uint32
    ALU = mybir.AluOpType
    ACT = mybir.ActivationFunctionType
    AX = mybir.AxisListType

    ctx = ExitStack()
    with ctx:
        def sb(name, shape, dt=f32, stack=ctx):
            return stack.enter_context(nc.sbuf_tensor(name, shape, dt))

        X = sb("X", [128, 16, D])
        RR = sb("RR", [128, 31232], f32r)
        R1, R2 = RR[:, 0:21504], RR[:, 21504:31232]
        stage = sb("stage", [128, 2, 768])
        xf = sb("xf", [128, 2, GT])
        xh = sb("xh", [128, 2, 2, GT], f32r)
        xl = sb("xl", [128, 2, 2, GT], f32r)
        cst = sb("cst", [128, 256])
        ident, upper = cst[:, 0:128], cst[:, 128:256]
        ones = sb("ones", [128, 128])
        IDX = sb("IDX", [128, 2, 2, 8], u32)
        OFF = sb("OFF", [1, 2, 24], i32)
        IDT = sb("IDT", [128, 2, NT], u32)
        TID = sb("TID", [128, 16])
        W2 = sb("W2", [128, 32])
        gw = sb("gw", [128, 2, NE])
        wiw = sb("wiw", [128, 2, NH])
        PA = sb("PA", [128, 2816])
        st = sb("st", [128, 16, 6])
        mv = sb("mv", [128, 16, 2])
        nt = sb("nt", [128, 16, 4])
        PS = [ctx.enter_context(nc.psum_tensor(f"ps{i}", [128, 512], f32)) for i in range(8)]
        def dram(name, shape, dt=f32):
            return nc.dram_tensor(name, shape, dt, kind="Internal").ap()

        xnd = [dram(f"xnd{n}", [T, D]) for n in range(2)]
        tabs = [[dram(f"tab{n}{h}", [128 * NT, 1]) for h in range(2)] for n in range(2)]
        ysd = [[dram(f"ysd{n}{h}", [128 * NT, D]) for h in range(2)] for n in range(2)]
        prog = {e: [] for e in ("pe", "act", "dve", "pool", "sp")}
        count = {}
        last_of = {}

        def carve(arena, at, shape):
            v = arena[:, at:at + int(np.prod(shape))]
            if len(shape) == 2:
                v = v.rearrange("p (a b) -> p a b", b=shape[1])
            elif len(shape) == 3:
                v = v.rearrange("p (a b c) -> p a b c", b=shape[1], c=shape[2])
            return v

        def op(eng, fn, waits=(), sem=None, dma=False):
            inc = 16 if eng == "sp" or dma else 1
            if sem is None:
                sem = eng
            count[sem] = count.get(sem, 0) + inc
            if not dma:
                last_of[eng] = (sem, count[sem])
            prog[eng].append((fn, list(waits), sem, inc))
            return (sem, count[sem])

        def quiet(eng, fn, waits=()):
            prog[eng].append((fn, list(waits), None, 0))

        def pe(sem, waits, mms):
            for n, (o, l, r, start, stop) in enumerate(mms):
                def fn(e, o=o, l=l, r=r, start=start, stop=stop):
                    return e.matmul(o, l, r, start=start, stop=stop, skip_group_check=True)
                w = waits if n == 0 else ()
                if n == len(mms) - 1:
                    return op("pe", fn, w, sem)
                quiet("pe", fn, w)

        def three(o, pairs, first=True, last=True):
            seq = [q for lh, ll, rh, rl in pairs for q in ((lh, rh), (lh, rl), (ll, rh))]
            return [(o, a, b, first and i == 0, last and i == len(seq) - 1) for i, (a, b) in enumerate(seq)]

        def f(ap):
            return ap.bitcast(f32)

        def copy(eng, o, i, waits, sem=None):
            if eng == "act":
                return op("act", lambda e: e.activation(o, i, ACT.Copy), waits, sem)
            return op(eng, lambda e: e.tensor_copy(o, i), waits, sem)

        def tt(eng, o, a, b, alu, waits, sem=None):
            return op(eng, lambda e: e.tensor_tensor(o, a, b, alu), waits, sem)

        def load(dst, src, waits, sem):
            return op("sp", lambda e: e.dma_start(dst, src), waits, sem)

        XT = [None] * NG
        XT[0] = load(X[:, 0:4, :], x[0:512, :].rearrange("(t p) d -> p t d", p=128), [], "x0")
        t_id = load(cst[:], cst_in, [], "c0")
        t_gw = load(gw[:], gw_in.rearrange("p (c e) -> p c e", c=2), [], "c1")

        stage_free = [[], []]
        nst = [0]

        def weight(src, n, dst, waits=(), eh="act", el="dve"):
            return split(bring(src, n), n, dst, waits, eh, el)

        def bring(src, n):
            s = nst[0] % 2
            nst[0] += 1
            return s, load(stage[:, s, 0:n], src, stage_free[s], f"w{s}")

        def split(brought, n, dst, waits=(), eh="act", el="dve"):
            s, t = brought
            hi, lo = dst[:, 0:n], dst[:, n:2 * n]
            a = copy(eh, hi, stage[:, s, 0:n], [t, *waits], "split_" + eh)
            b = tt(el, lo, stage[:, s, 0:n], f(hi), ALU.subtract, [a], "split_" + el)
            stage_free[s] = [b]
            return b

        def moments(first, count, at, waits, eng):
            for i in range(count):
                w = waits[i // 4] if i % 4 == 0 else []
                t = op("dve", lambda e, i=i: e.bn_stats(st[:, at + i, :], X[:, first + i, :]), w)
            for i in range(count):
                t = op("dve", lambda e, i=i: e.bn_aggr(mv[:, at + i, :], st[:, at + i, :]), [t] if i == 0 else [])
            q = slice(at, at + count)
            a, b, y, v = nt[:, q, 0], nt[:, q, 1], nt[:, q, 3], mv[:, q, 1]
            t = op("dve", lambda e: e.tensor_scalar(a, v, EPS, None, ALU.add), [t])
            t = op("dve", lambda e: e.tensor_scalar(b.bitcast(i32), a.bitcast(i32), 1, None,
                                                    ALU.logical_shift_right), [t])
            t = op("dve", lambda e: e.tensor_scalar(y.bitcast(i32), b.bitcast(i32), -1.0, float(0x5f3759df),
                                                    ALU.mult, ALU.add), [t])
            for _ in range(3):
                t = tt(eng, b, y, y, ALU.mult, [t])
                t = tt(eng, b, b, a, ALU.mult, [t])
                t = op(eng, lambda e: e.tensor_scalar(b, b, -0.5, 1.5, ALU.mult, ALU.add), [t])
                t = tt(eng, y, y, b, ALU.mult, [t])
            return t

        def centre(g, at, t, xn, xn_free, eng):
            for i in range(4):
                t = op(eng, lambda e, i=i: e.tensor_scalar(xn[:, i, :], X[:, 4 * g + i, :], mv[:, at + i, 0:1],
                                                           nt[:, at + i, 3:4], ALU.subtract, ALU.mult),
                       [t] + xn_free if i == 0 else [], "xn_" + eng)
            return t

        def norm(g, ready, xn, xn_free, eng="dve"):
            return centre(g, 0, moments(4 * g, 4, 0, [ready], eng), xn, xn_free, eng)

        xbuf_free = [[], []]

        def flip(g, xn, t_xn, banks, bank_free, xf_free=()):
            pts = []
            for dc in range(2):
                for i in range(4):
                    o, s = PS[banks[dc]][:, 128 * i:128 * i + 128], xn[:, i, 128 * dc:128 * dc + 128]
                    fn = lambda e, o=o, s=s: e.transpose(o, s, ident)
                    w = ([t_xn, t_id] if dc == 0 else []) + bank_free[dc] if i == 0 else []
                    if i == 3:
                        pts.append(op("pe", fn, w, "pe_xt"))
                    else:
                        quiet("pe", fn, w)
            b = g % 2
            for dc in range(2):
                ta = copy("act", xf[:, dc, :], PS[banks[dc]][:, :], [pts[1], *xf_free], "xf")
            th = copy("dve", xh[:, b, :, :], xf[:, :, :], [ta] + xbuf_free[b], "xh")
            tl = tt("dve", xl[:, b, :, :], xf[:, :, :], f(xh[:, b, :, :]), ALU.subtract, [th], "xl")
            return ta, th, tl, pts[1]

        def gather(dst, src, idx, waits, sem):
            return op("pool", lambda e: e.indirect_dma_start(
                out=dst, out_offset=None, in_=src, in_offset=bass.IndirectOffsetOnAxis(ap=idx, axis=0)),
                waits, sem, dma=True)

        t_ones = op("pool", lambda e: e.memset(ones[:], 1.0), [])
        t_tid = load(TID[:], tok_in, [], "c4")
        zeroed = {}

        class Moe:

            def __init__(self, n, PA, ready, on_group, free, edge, xf_free):
                self.n, self.places = n, PLACES[n]
                self.xnd, self.tabs, self.out = xnd[n], tabs[n], ysd[n]
                self.ready, self.on_group, self.free, self.edge = ready, on_group, free, edge
                self.flips, self.small, self.eng = (1, 2), 0, "pool"
                F = lambda at, *shape: carve(PA, at, shape)
                self.XN = F(0, 4, D)
                b = 1024
                v = {}
                for name, shape in (("LG", (8, NE)), ("EX", (8, NE)), ("SEL", (8, NE)), ("C", (8, NE)), ("MS", (8, NE)),
                                    ("CS", (9, NE)), ("RK", (8, NE)), ("NTI", (NE,)), ("NTF", (NE,)), ("BE", (NE,)),
                                    ("IB", (NE,)), ("mx", (8,)), ("sm", (8,)), ("SH", (8,)), ("SS", (8,)),
                                    ("G1", (4, 64)), ("G2", (4, 64)), ("ROW", (248,)),
                                    ("SL", (2, 128))):
                    v[name] = F(b, *shape)
                    b += int(np.prod(shape))
                assert b <= PA.shape[1], b
                self.LG, self.EX, self.SEL, self.C, self.MS = v["LG"], v["EX"], v["SEL"], v["C"], v["MS"]
                self.CS, self.RK, self.NTI, self.NTF, self.BE = v["CS"], v["RK"], v["NTI"], v["NTF"], v["BE"]
                self.IB, self.mx, self.sm, self.SH, self.SS = v["IB"], v["mx"], v["sm"], v["SH"], v["SS"]
                self.G1, self.G2, self.ROW, self.SL = v["G1"], v["G2"], v["ROW"], v["SL"]
                self.t_row = load(self.ROW, row_in, edge, "row")
                self.XR, self.nt = {}, {}
                self.xn_free, self.xf_free = list(edge), list(xf_free)
                self.lg = {}
                self.stored = []
                self.off, self.idt, self.idx, self.w2, self.tab = {}, {}, {}, {}, {}
                self.ysd = {}
                self.left = {g: 5 for g in range(NG)}
                self.experts = []
                self.wrote = {}
                self.fetched = None
                self.moments = {}

            def settle(self, FA, RA, edge):
                F = lambda at, *shape: carve(FA, at, shape)
                self.SM_ = F(0, 2, GT)
                self.TM = F(1024, 2, GT)
                self.XS = [F(3584, D), F(3840, D), F(4096, D), F(0, D)]
                self.S = F(1024, 2, 176)
                self.G = F(1376, 2, 176)
                self.YS = F(2048, 2, D)
                self.GA = F(2560, 2, 2, D)
                self.GH = carve(RA, 0, (3, GT))
                self.GL = carve(RA, 1536, (3, GT))
                self.XTH = carve(RA, 0, (3, D))
                self.XTL = carve(RA, 768, (3, D))
                self.GTH = carve(RA, 1536, (2, D))
                self.GTL = carve(RA, 2048, (2, D))
                self.edge = edge
                self.sm_free = [list(edge), list(edge)]
                self.tm_free = [list(edge), list(edge)]
                self.gh_free = [list(edge) for _ in range(3)]
                self.xs_free = [list(edge) for _ in range(4)]
                self.xt_free = [list(edge) for _ in range(3)]
                self.s_free = [list(edge), list(edge)]
                self.gt_free = [list(edge), list(edge)]
                self.ys_free = [list(edge), list(edge)]
                self.ga_free = [list(edge), list(edge)]
                self.flips, self.small, self.eng = (6, 7), 6, "dve"

            def norm(self, g):
                if g in self.moments:
                    self.nt[g] = centre(g, 4 * g, self.moments[g], self.XN, self.xn_free, self.eng)
                    return
                self.nt[g] = norm(g, self.ready(g) + self.edge, self.XN, self.xn_free, self.eng)

            def flip(self, g):
                free = self.free
                t = load(self.xnd[512 * g:512 * g + 512, :].rearrange("(t p) d -> p t d", p=128), self.XN,
                         [self.nt[g]], f"xnd{g % 2}")
                self.stored.append(t)
                self.xn_free = [t]
                pts = []
                for dc, bank in enumerate(self.flips):
                    for i in range(4):
                        o, q = PS[bank][:, 128 * i:128 * i + 128], self.XN[:, i, 128 * dc:128 * dc + 128]
                        fn = lambda e, o=o, q=q: e.transpose(o, q, ident)
                        w = [self.nt[g], t_id] + free[bank] if i == 0 else []
                        if i == 3:
                            pts.append(op("pe", fn, w, "pe_xt"))
                        else:
                            quiet("pe", fn, w)
                for dc, bank in enumerate(self.flips):
                    ta = copy("act", xf[:, dc, :], PS[bank][:, :], [pts[dc], *self.xf_free], "xf")
                    free[bank] = [ta]
                self.XR[g] = [ta, None, None]
                self.xn_free = self.xn_free + [pts[1]]

            def halves(self, g):
                b, ta = g % 2, self.XR[g][0]
                th = copy("dve", xh[:, b, :, :], xf[:, :, :], [ta] + xbuf_free[b], "xh")
                tl = tt("dve", xl[:, b, :, :], xf[:, :, :], f(xh[:, b, :, :]), ALU.subtract, [th], "xl")
                self.XR[g] = [ta, th, tl]
                self.xf_free = self.xf_free + [tl]

            def logits(self, g):
                free, o = self.free, 4 * (g % 2)
                ta = self.XR[g][0]
                mms = [(PS[self.small][:, NE * i:NE * i + NE], xf[:, dc, 128 * i:128 * i + 128], gw[:, dc, :], dc == 0, dc == 1)
                       for i in range(4) for dc in range(2)]
                tg = pe("pe_gate", [ta, t_gw] + free[self.small], mms)
                self.xf_free = [tg]
                LG, G1, G2 = self.LG[:, o:o + 4, :], self.G1, self.G2
                t = copy("dve", LG, PS[self.small][:, 0:32].rearrange("p (t e) -> p t e", e=NE), [tg] + self.lg.get("free", []))
                free[self.small] = [t]
                four = [128, 4, NE, NE]
                j_ = LG.rearrange("p t (o e) -> p t o e", o=1).to_broadcast(four)
                e_ = LG.rearrange("p t (e o) -> p t e o", o=1).to_broadcast(four)
                v = lambda a: a.rearrange("p t (e j) -> p t e j", j=NE)
                t1 = tt("dve", v(G1), j_, e_, ALU.is_gt, [t])
                t2 = tt("dve", v(G2), j_, e_, ALU.is_ge, [])
                less = self.ROW[:, 184:248]
                lb = less.rearrange("p (o n) -> p o n", o=1).to_broadcast([128, 4, 64])
                t2 = tt("dve", G2, G2, lb, ALU.mult, [t2, self.t_row])
                t2 = tt("dve", G1, G1, G2, ALU.max, [t2])
                RK = self.RK[:, o:o + 4, :]
                t2 = op("dve", lambda e: e.tensor_reduce(RK, v(G1), AX.X, ALU.add), [t2])
                self.lg[g] = t2

            def choose(self, h):
                LG, EX, SEL, C, RK, mx, sm, CS = (self.LG, self.EX, self.SEL, self.C, self.RK, self.mx, self.sm, self.CS)
                bc = lambda a: a.rearrange("p (t o) -> p t o", o=1).to_broadcast([128, 8, NE])
                t = op("dve", lambda e: e.tensor_scalar(SEL, RK, 2.0, None, ALU.is_lt), [self.lg[2 * h + 1]])
                tc = op("dve", lambda e: e.memset(CS[:, 0, :], 0.0), [])
                ts = op("dve", lambda e: e.tensor_reduce(mx, LG, AX.X, ALU.max), [])
                ts = tt("dve", EX, LG, bc(mx), ALU.subtract, [ts])
                te = op("act", lambda e: e.activation(EX, EX, ACT.Exp), [ts])
                for i in range(8):
                    tc = tt("dve", CS[:, i + 1, :], CS[:, i, :], SEL[:, i, :], ALU.add, [tc, t])
                self.counted = tc
                t = op("dve", lambda e: e.tensor_reduce(sm, EX, AX.X, ALU.add), [te])
                t = op("dve", lambda e: e.reciprocal(sm, sm), [t])
                t = tt("dve", EX, EX, bc(sm), ALU.mult, [t])
                self.weighed = op("dve", lambda e: e.scalar_tensor_tensor(C, EX, 0.5, SEL, ALU.mult, ALU.mult), [t])

            def count(self, h):
                CS, SEL = self.CS, self.SEL
                tp = pe("pe_gate", [self.counted, t_id, t_ones] + self.free[self.small],
                        [(PS[self.small][:, 0:72], ones[:], CS.rearrange("p t e -> p (t e)"), True, False),
                         (PS[self.small][:, 0:64], upper, SEL.rearrange("p t e -> p (t e)"), False, True)])
                self.placed = (tp, self.weighed)

            def place(self, h):
                SEL, C, MS, LG, NTI, NTF, BE, IB, SH, SS, ROW = (
                    self.SEL, self.C, self.MS, self.LG, self.NTI, self.NTF, self.BE, self.IB, self.SH, self.SS, self.ROW)
                tp, tw = self.placed
                bc = lambda a: a.rearrange("p (t o) -> p t o", o=1).to_broadcast([128, 8, NE])
                ts = lambda o, i, a, b, o1, o2, w: op("dve", lambda e: e.tensor_scalar(o, i, a, b, o1, o2), w)
                nti = NTI.bitcast(i32)
                t = ts(nti, PS[self.small][:, 64:72], 127.0, None, ALU.add, ALU.bypass, [tp])
                t = ts(nti, nti, 7, None, ALU.logical_shift_right, ALU.bypass, [t])
                t = copy("dve", NTF, nti, [t])
                m = self.G1[:, 0, :].rearrange("p (e j) -> p e j", j=NE)
                less = ROW[:, 184:248].rearrange("p (e j) -> p e j", j=NE)
                t = tt("dve", m, less, NTF.rearrange("p (o j) -> p o j", o=1).to_broadcast([128, NE, NE]), ALU.mult, [t])
                t = op("dve", lambda e: e.tensor_reduce(BE, m, AX.X, ALU.add), [t])
                ti = tt("dve", IB, BE, NTF, ALU.add, [t])
                t = ts(BE, BE, 128.0, 1.0, ALU.mult, ALU.add, [ti])
                pos = PS[self.small][:, 0:64].rearrange("p (t e) -> p t e", e=NE)
                t = tt("dve", MS, pos, BE.rearrange("p (o e) -> p o e", o=1).to_broadcast([128, 8, NE]), ALU.add, [t])
                self.free[self.small] = [t]
                t = tt("dve", MS, MS, SEL, ALU.mult, [t])
                t1 = op("dve", lambda e: e.tensor_reduce(SH, MS, AX.X, ALU.max), [t])
                t2 = op("dve", lambda e: e.tensor_reduce(SS, MS, AX.X, ALU.add), [])
                idx = IDX[:, h, :, :]
                t1 = ts(idx[:, 0, :], SH, -1.0, None, ALU.add, ALU.bypass, [t1])
                t2 = op("dve", lambda e: e.scalar_tensor_tensor(idx[:, 1, :], SS, -1.0, SH, ALU.add, ALU.subtract), [t2])
                self.idx[h] = t2
                w2 = W2[:, :].rearrange("p (h k t) -> p h k t", h=2, k=2)
                t = tt("dve", LG, MS, bc(SH), ALU.is_equal, [tw])
                t = tt("dve", LG, LG, C, ALU.mult, [t])
                t3 = op("dve", lambda e: e.tensor_reduce(w2[:, h, 0, :], LG, AX.X, ALU.add), [t])
                t = tt("dve", C, C, LG, ALU.subtract, [t])
                t = op("dve", lambda e: e.tensor_reduce(w2[:, h, 1, :], C, AX.X, ALU.add), [t])
                self.w2[h] = t
                cm = self.G2[0:1, :, :].rearrange("p a b -> p (a b)")[:, 0:7 * NT].rearrange("p (j e) -> p j e", e=7)
                jv = ROW[0:1, 0:161].rearrange("p (j e) -> p j e", e=7)
                ibv = IB[0:1, 0:7].rearrange("p (o e) -> p o e", o=1).to_broadcast([1, NT, 7])
                o = 161 + 7 * self.n
                st_ = ROW[0:1, o:o + 7].rearrange("p (o e) -> p o e", o=1).to_broadcast([1, NT, 7])
                t = tt("dve", cm, ibv, jv, ALU.is_le, [t, self.t_row])
                t = tt("dve", cm, cm, st_, ALU.mult, [t])
                offf = self.EX[0:1, :, :].rearrange("p a b -> p (a b)")[:, 0:NT]
                t = op("dve", lambda e: e.tensor_reduce(offf, cm, AX.X, ALU.add), [t])
                self.off[h] = ts(OFF[0:1, h, 0:NT], offf, float(self.places[0]), None, ALU.add, ALU.bypass, [t])
                self.lg["free"] = [self.off[h]]
                self.t1 = t1

            def scatter(self, h, n):
                i, k = divmod(n, 2)
                t = op("pool", lambda e: e.indirect_dma_start(
                    out=self.tabs[h], out_offset=bass.IndirectOffsetOnAxis(ap=IDX[:, h, k, i:i + 1], axis=0),
                    in_=TID[:, 8 * h + i:8 * h + i + 1], in_offset=None),
                    [self.t1, self.idx[h], t_tid, zeroed[self.n, h]] if n == 0 else [], f"tab{h}", dma=True)
                self.tab[h] = t

            def load_slots(self, h):
                self.tab[h] = load(self.SL[0:NT, h, :], self.tabs[h].rearrange("(a p) o -> a (p o)", p=128),
                                   [self.tab[h]], f"slot{h}")

            def turn_ids(self, h):
                t = pe("pe_gate", [self.tab[h], t_id] + self.free[self.small],
                       [(PS[self.small][:, 0:NT], self.SL[0:NT, h, :], ident[0:NT, 0:NT], True, True)])
                t = copy("dve", IDT[:, h, :], PS[self.small][:, 0:NT], [t])
                self.free[self.small] = self.idt[h] = [t]

            def shared(self, groups, slots, wt, between):
                free = self.free
                tasks = [(g, i) for g in groups for i in range(3)]
                queue, lo = {}, None
                for s, (g, i) in enumerate(tasks + [(None, None)] * 2):
                    if g is not None:
                        w = slots[i]
                        ta, th, tl = self.XR[g]
                        b = g % 2
                        toks = []
                        for z in range(2):
                            bk = 2 * z + s % 2
                            pairs = [(w[:, z * 256 + dc * 128:z * 256 + dc * 128 + 128],
                                      w[:, 768 + z * 256 + dc * 128:768 + z * 256 + dc * 128 + 128],
                                      xh[:, b, dc, :], xl[:, b, dc, :]) for dc in range(2)]
                            toks.append(pe("pe_gu", [th, tl, wt[i]] + free[bk], three(PS[bk][:, :], pairs)))
                        if i == 2:
                            xbuf_free[b] = [toks[1]]
                        k2, k3 = s % 2, s % 3
                        S, TM, GH, GL = self.SM_[:, k2, :], self.TM[:, k2, :], self.GH[:, k3, :], self.GL[:, k3, :]
                        t = op("act", lambda e, S=S, gb=s % 2: e.activation(S, PS[gb][:, :], ACT.Silu),
                               [toks[0]] + self.sm_free[k2], "silu")
                        free[s % 2] = [t]
                        t = tt("dve", TM, S, PS[2 + s % 2][:, :], ALU.mult, [t, toks[1]] + self.tm_free[k2])
                        free[2 + s % 2] = [t]
                        self.sm_free[k2] = [t]
                    if lo is not None:
                        lo()
                        lo = None
                    if g is not None:
                        t1 = copy("act", GH, TM, [t] + self.gh_free[k3], "gh")

                        def lo(s=s, g=g, i=i, k2=k2, k3=k3, GL=GL, GH=GH, TM=TM, t1=t1):
                            t2 = tt("dve", GL, TM, f(GH), ALU.subtract, [t1, *self.gh_free[k3]], "gl")
                            self.tm_free[k2] = [t2]
                            queue[s] = (g, i, [t1, t2], k3)
                    if s - 2 in queue:
                        self.shared_down(slots, *queue.pop(s - 2))
                    if between:
                        between.pop(0)()
                for lst in (self.xs_free[3:], self.s_free, self.xt_free, self.gt_free):
                    for q in lst:
                        q += [last_of["dve"], last_of["pe"]]

            def shared_down(self, slots, g, i, toks, k3):
                w, free = slots[i], self.free
                for a in range(4):
                    bk = 4 + a // 2
                    y = PS[bk][:, 256 * (a % 2):256 * (a % 2) + 256]
                    sl = slice(128 * a, 128 * a + 128)
                    mms = [(y, self.GH[:, k3, sl], w[:, 512:768]), (y, self.GH[:, k3, sl], w[:, 1280:1536]),
                           (y, self.GL[:, k3, sl], w[:, 512:768])]
                    mms = [(*m, i == 0 and a % 2 == 0 and q == 0, i == 2 and q == 2) for q, m in enumerate(mms)]
                    wts = (toks if a == 0 else []) + (free[bk] if i == 0 else [])
                    t = pe("pe_down", wts, mms)
                self.gh_free[k3] = [t]
                if i == 2:
                    for b in range(2):
                        xs = X[:, 4 * g + 2 * b:4 * g + 2 * b + 2, :]
                        y = PS[4 + b][:, :].rearrange("p (t d) -> p t d", d=D)
                        tx = op("dve", lambda e, xs=xs, y=y: e.scalar_tensor_tensor(xs, y, 0.5, xs, ALU.mult, ALU.add),
                                [t] + [self.wrote[q] for q in (4 * g + 2 * b, 4 * g + 2 * b + 1) if q in self.wrote],
                                "xres")
                        free[4 + b] = [tx]
                        self.wrote[4 * g + 2 * b] = self.wrote[4 * g + 2 * b + 1] = tx
                    self.done(g, tx)

            def done(self, g, t):
                self.left[g] -= 1
                if self.left[g] == 0:
                    self.on_group(g, t)

            def fetch_x(self, j):
                h, q = divmod(j, NT)
                k = j % 4
                return gather(self.XS[k], self.xnd, IDT[:, h, q:q + 1],
                              [*self.idt[h], *self.stored] + self.xs_free[k], f"xs{k}")

            def prefetch(self):
                self.xs = {j: self.fetch_x(j) for j in range(3)}

            def sparse(self, between):
                free = self.free
                regs, xt, gt = {}, {}, {}
                xs = self.xs

                def turn_x(j):
                    k = j % 3
                    for dc in range(2):
                        fn = lambda e, dc=dc: e.transpose(PS[0][:, 128 * dc:128 * dc + 128],
                                                          self.XS[j % 4][:, 128 * dc:128 * dc + 128], ident)
                        if dc == 0:
                            quiet("pe", fn, [xs[j], t_id] + free[0])
                        else:
                            t = op("pe", fn, [], "pe_t")
                    self.xs_free[j % 4] = [t]
                    th = copy("act", self.XTH[:, k, :], PS[0][:, 0:256], [t] + self.xt_free[k], "xth")
                    tl = tt("dve", self.XTL[:, k, :], PS[0][:, 0:256], f(self.XTH[:, k, :]), ALU.subtract,
                            [th] + self.xt_free[k], "xtl")
                    free[0] = [tl]
                    xt[j] = [th, tl]

                def hidden(j):
                    k, bk, ks = j % 3, 1 + j % 2, j % 2
                    h, t = divmod(j, NT)

                    def take(e, t=t):
                        regs[j] = e.value_load(OFF[0:1, h, t:t + 1], min_val=0, max_val=max(self.places))

                    prog["pe"].append((take, [self.off[h]], None, 0))
                    seq = []
                    for dc in range(2):
                        H, L = (a[:, k, 128 * dc:128 * dc + 128] for a in (self.XTH, self.XTL))
                        seq += [(H, 352 * dc), (H, 704 + 352 * dc), (L, 352 * dc)]
                    for q, (l, o) in enumerate(seq):
                        fn = lambda e, l=l, o=o, q=q: e.matmul(PS[bk][:, 0:352], l, RR[:, bass.ds(regs[j] + o, 352)],
                                                               start=q == 0, stop=q == 5, skip_group_check=True)
                        if q == 5:
                            t = op("pe", fn, [], "pe_h")
                        else:
                            quiet("pe", fn, xt[j] + self.experts + free[bk] if q == 0 else [])
                    self.xt_free[k] = [t]
                    ts = op("act", lambda e: e.activation(self.S[:, ks, :], PS[bk][:, 0:176], ACT.Silu),
                            [t] + self.s_free[ks], "silu")
                    tm = tt("dve", self.G[:, ks, :], self.S[:, ks, :], PS[bk][:, 176:352], ALU.mult,
                            [ts] + self.s_free[ks])
                    free[bk] = [tm]
                    gt[j] = [tm]

                def turn_g(j):
                    ks = j % 2
                    for z in range(2):
                        fn = lambda e, z=z: e.transpose(PS[3][0:88, 128 * z:128 * z + 128],
                                                        self.G[:, ks, 88 * z:88 * z + 88], ident)
                        if z == 0:
                            quiet("pe", fn, gt[j] + free[3])
                        else:
                            t = op("pe", fn, [], "pe_t")
                    self.s_free[ks] = [t]
                    th = copy("act", self.GTH[0:88, ks, :], PS[3][0:88, 0:256], [t] + self.gt_free[ks], "gth")
                    tl = tt("dve", self.GTL[0:88, ks, :], PS[3][0:88, 0:256], f(self.GTH[0:88, ks, :]), ALU.subtract,
                            [th] + self.gt_free[ks], "gtl")
                    free[3] = [tl]
                    gt[j] = [th, tl]

                def down(j):
                    ks, bk = j % 2, 4 + j % 2
                    seq = []
                    for z in range(2):
                        H, L = (a[0:88, ks, 128 * z:128 * z + 128] for a in (self.GTH, self.GTL))
                        seq += [(H, 1408 + 256 * z), (H, 1920 + 256 * z), (L, 1408 + 256 * z)]
                    for q, (l, o) in enumerate(seq):
                        fn = lambda e, l=l, o=o, q=q: e.matmul(PS[bk][:, 0:256], l, RR[0:88, bass.ds(regs[j] + o, 256)],
                                                               start=q == 0, stop=q == 5, skip_group_check=True)
                        if q == 5:
                            t = op("pe", fn, [], "pe_d")
                        else:
                            quiet("pe", fn, gt[j] + free[bk] if q == 0 else [])
                    self.gt_free[ks] = [t]
                    t = copy("dve" if j % 2 else "act", self.YS[:, ks, :], PS[bk][:, 0:256], [t] + self.ys_free[ks],
                             "ys" + "ab"[j % 2])
                    free[bk] = [t]
                    h, q = divmod(j, NT)
                    t = load(self.out[h][128 * q:128 * q + 128, :], self.YS[:, ks, :], [t], f"yst{ks}")
                    self.ys_free[ks] = [t]
                    self.ysd[h, ks] = t

                turn_x(0)
                turn_x(1)
                for j in range(2 * NT + 2):
                    if j + 3 < 2 * NT:
                        xs[j + 3] = self.fetch_x(j + 3)
                    if j < 2 * NT:
                        hidden(j)
                    if 0 <= j - 1 < 2 * NT:
                        turn_g(j - 1)
                    if j >= 2:
                        down(j - 2)
                    if j + 2 < 2 * NT:
                        turn_x(j + 2)
                    if between:
                        between.pop(0)()
                for lst in (self.sm_free, self.tm_free, self.gh_free):
                    for q in lst:
                        q += [last_of["dve"], last_of["pe"]]

            def collect(self, h, i):
                k = i % 2
                ts = [gather(self.GA[:, k, r, :], self.out[h], IDX[:, h, r, i:i + 1],
                             [self.ysd[h, 0], self.ysd[h, 1], self.idx[h]] + self.ga_free[k], f"ga{k}{r}")
                      for r in range(2)]
                self.add()
                self.fetched = (h, i, ts)

            def add(self):
                if self.fetched is None:
                    return
                h, i, ts = self.fetched
                self.fetched = None
                k, tile = i % 2, 8 * h + i
                w2 = W2[:, :].rearrange("p (h k t) -> p h k t", h=2, k=2)
                for r in range(2):
                    row = self.GA[:, k, r, :]
                    tx = op("dve", lambda e, r=r, row=row: e.scalar_tensor_tensor(
                        X[:, tile, :], row, w2[:, h, r, i:i + 1], X[:, tile, :], ALU.mult, ALU.add),
                        [ts[r], self.w2[h]] + ([self.wrote[tile]] if tile in self.wrote else []), "xres")
                    self.wrote[tile] = tx
                self.ga_free[k] = [tx]
                self.done(tile // 4, tx)

        fs = ExitStack()
        xn = xf[:, :, :].rearrange("p c (t d) -> p (c t) d", d=D)
        xres = [None] * NG
        XR, normed, late, brought1 = {}, {}, {}, {}
        slots1 = [RR[:, 1536 * i:1536 * i + 1536] for i in range(3)]
        parts1 = [(e, p) for e in range(NE) for p in range(2)]

        def after_group1(g, t):
            xres[g] = t

        def filler(*fs):
            def go():
                for q in fs:
                    q()
            return go

        def part(e, p, n):
            w, o = (704, 0) if p == 0 else (512, 704)
            at = PLACES[n][e] + 2 * o
            return wex_in[e][:, o:o + w], w, RR[:, at:at + 2 * w]

        def ahead1(i):
            for q in parts1[2 * i - 2:2 * i] if i else []:
                m1.experts.append(split(brought1.pop(q), *part(*q, 0)[1:], (), "act", "pool" if i < 4 else "dve"))
            for q in parts1[2 * i:2 * i + 2]:
                brought1[q] = bring(*part(*q, 0)[:2])

        m1 = Moe(0, PA, lambda g: [XT[g]], after_group1, {k: [] for k in range(8)}, [], [])
        m1.settle(sb("FA1", [128, 4352], f32, fs), sb("RA1", [128, 3072], f32r, fs), [])
        zero = m1.GA[0:NT, 0, 0, 0:128]
        t_zero = op("pool", lambda e: e.memset(zero, 0.0), [])
        m1.norm(0)
        wt1 = [weight(wsh_in[0], 768, slots1[0])]
        XT[1] = load(X[:, 4:8, :], x[512:1024, :].rearrange("(t p) d -> p t d", p=128), [], "x1")
        m1.flip(0)
        wt1 += [weight(wsh_in[i], 768, slots1[i]) for i in (1, 2)]
        m1.halves(0)
        m1.logits(0)
        for g in (2, 3):
            XT[g] = load(X[:, 4 * g:4 * g + 4, :], x[512 * g:512 * g + 512, :].rearrange("(t p) d -> p t d", p=128),
                         [], f"x{g}")
        for n in range(2):
            for h in range(2):
                zeroed[n, h] = load(tabs[n][h].rearrange("(a p) o -> a (p o)", p=128), zero, [t_zero], f"z{n}{h}")

        m1.ga_free[0] = list(zeroed.values())

        def scatters(m, h):
            for n in range(16):
                m.scatter(h, n)

        t_iw = load(wiw[:], wiw_in.rearrange("p (c e) -> p c e", c=2), [], "c3")

        def small1():
            late["small"] = weight(ws_in, 768, R2[:, 8192:9728])

        m1.norm(1)

        def moments1():
            t = moments(8, 8, 8, [[XT[2]], [XT[3]]], "dve")
            m1.moments = {2: t, 3: t}

        def scatter1(n):
            for q in range(4 * n, 4 * n + 4):
                m1.scatter(0, q)

        prep1 = [[lambda: m1.flip(1), moments1, lambda: m1.norm(2)], [lambda: m1.halves(1), lambda: m1.logits(1)],
                 [lambda: m1.choose(0)], [lambda: m1.flip(2), lambda: m1.count(0)],
                 [lambda: m1.place(0), lambda: m1.halves(2), lambda: m1.norm(3), lambda: scatter1(0)],
                 [lambda: m1.logits(2), lambda: scatter1(1)], [lambda: m1.flip(3), lambda: scatter1(2)],
                 [lambda: m1.halves(3), lambda: m1.logits(3), lambda: scatter1(3)],
                 [lambda: m1.load_slots(0), lambda: m1.choose(1)], [lambda: m1.turn_ids(0), m1.prefetch],
                 [lambda: m1.count(1)]]
        m1.shared([0, 1, 2], slots1, wt1, [filler(lambda i=i: ahead1(i), *p) if i < 9 else filler(*p)
                                           for i, p in enumerate(prep1)])
        wqi_brought = {}

        def ahead_wqi(k, n, waits=()):
            if n is not None:
                late[f"wqi{n}"] = split(wqi_brought.pop(n), 512, R2[:, 1024 * n:1024 * n + 1024], waits)
            if k is not None:
                wqi_brought[k] = bring(wqi_in[k], 512)

        def attention_norm():
            normed[0] = norm(0, [xres[0]], xn, m1.xf_free)

        def attention_flip():
            XR[0] = flip(0, xn, normed[0], (6, 7), [m1.free[6], m1.free[7]])
            m1.free[6] = m1.free[7] = [XR[0][0]]

        def moments_of_1():
            late["moments"] = moments(4, 4, 4, [[xres[1]]], "pool")

        def routing_fills(m):
            fills = {18: [lambda: m.load_slots(1)],
                     19: [lambda: m.turn_ids(1)], 44: [m.add]}
            fills |= {2 + n: [lambda n=n: m.scatter(1, n)] for n in range(16)}
            fills |= {28 + 2 * i: [lambda i=i: m.collect(0, i)] for i in range(8)}
            return fills

        fill1 = routing_fills(m1)
        fill1[0] = [lambda: m1.place(1)]
        fill1[22] = [small1]
        fill1[37] = [attention_norm]
        fill1[43] = [attention_flip]
        for i, (k, n) in enumerate(zip([3, 4, 5, 6, 7, None], [None, 3, 4, 5, 6, 7])):
            fill1[24 + 3 * i] = fill1.get(24 + 3 * i, []) + [lambda k=k, n=n: ahead_wqi(k, n)]
        m1.sparse([filler(*fill1.get(i, [])) for i in range(48)])
        sparse_done = [last_of["pe"]]
        m1.shared([3], slots1, wt1, [filler(lambda i=i: m1.collect(1, 2 * i), lambda i=i: m1.collect(1, 2 * i + 1),
                                            lambda i=i: ahead_wqi((0, 1, 2, None)[i], (None, 0, 1, 2)[i], sparse_done))
                                     for i in range(4)] +
                  [filler(m1.add, moments_of_1)])
        fs.close()
        edge = [last_of[e] for e in ("pe", "act", "dve")] + [t for q in m1.ys_free for t in q]
        t_small, t_wqi = late["small"], [late[f"wqi{k}"] for k in range(8)]

        fs = ExitStack()
        A = lambda name, shape, dt=f32: sb(name, shape, dt, fs)
        PTH = R1[:, 16384:17152].rearrange("p (h n) -> p h n", h=2)
        PTL = R1[:, 17152:17920].rearrange("p (h n) -> p h n", h=2)
        OH, OL = R1[:, 17920:18432], R1[:, 18432:18944]
        QIH = R1[:, 18944:19200].rearrange("p (b n) -> p b n", b=2)
        QIL = R1[:, 19200:19456].rearrange("p (b n) -> p b n", b=2)
        QH = R1[:, 19456:20480].rearrange("p (r b n) -> p r b n", r=4, b=2)
        QL = R1[:, 20480:21504].rearrange("p (r b n) -> p r b n", r=4, b=2)
        QF = A("QF", [128, 4, 2, 128])
        KF = A("KF", [128, 2, 128])
        KH, KL = A("KH", [128, GT], f32r), A("KL", [128, GT], f32r)
        VH, VL = A("VH", [128, 4, 128], f32r), A("VL", [128, 4, 128], f32r)
        SP = A("SP", [128, 2, 2, 384])
        IM = PA[:, 768:1536]
        W = [PA[:, 2048:2816], A("W", [128, 768])]
        M8 = A("M8", [128, 4, 8])
        MX = A("MX", [128, 2, 4])
        NB = A("NB", [128, 2, 4])
        SM = A("SM", [128, 2, 4])
        RC = A("RC", [128, 2, 4])
        KIF = carve(PA, 1536, (2, 128))
        KIH, KIL = A("KIH", [128, GT], f32r), A("KIL", [128, GT], f32r)
        R = A("R", [128, 2, 384])
        I = PA[:, 0:768]
        IW = A("IW", [128, 4, NH])
        QIF = carve(PA, 1792, (2, 128))
        QB, SB_, TB, OB, YB = 0, (1, 2), (3, 4), 5, (6, 7)
        free = m1.free
        t_wq = [weight(wq_in[k], 512, R1[:, 1024 * k:1024 * k + 1024], edge, "pool", "pool") for k in range(8)]
        t_wo = {k: weight(wo_in[k], 512, R1[:, 8192 + 1024 * k:8192 + 1024 * k + 1024], edge, "pool", "pool")
                for k in range(8)}
        xn_free = [[]]
        rf = {k: list(edge) for k in ("k", "w0", "w1", "im0", "im1", "im2", "im3", "o", "pt", "v", "sp0", "sp1",
                                      "q0", "q1", "q2", "q3", "qi", "ki", "iw", "r0", "r1")}
        rf |= {k: [] for k in ("i0", "i1", "i2", "i3")}
        TILES = [(b, h, 384 * b + 128 * h, 128 * (h + 1)) for b in range(2) for h in range(2)]

        def do_norm(g):
            normed[g] = norm(g, [xres[g]], xn, xn_free[0], "pool" if g > 1 else "dve")

        def small(kind, hl, dc):
            o = 8192 + 768 * hl + 256 * kind + 128 * dc
            return R2[:, o:o + 128]

        tk = {}

        def project(kind, g):
            b = g % 2
            _, th, tl, _ = XR[g]
            pairs = [(small(kind, 0, dc), small(kind, 1, dc), xh[:, b, dc, :], xl[:, b, dc, :]) for dc in range(2)]
            t = pe("pe_k", [th, tl, t_small] + free[QB], three(PS[QB][:, :], pairs))
            KX_F, KX_H, KX_L, name = ((KIF, KIH, KIL, "ki"), (KF, KH, KL, "k"))[kind]
            p2 = PS[QB][:, :].rearrange("p (b n) -> p b n", b=2)
            t1 = copy("act", KX_F[:, :, :], p2[:, :, 0:128], [t] + rf[name])
            t2 = copy("act", KX_H[:, :], PS[QB][:, :], rf[name], "kh")
            t3 = tt("dve", KX_L[:, :], PS[QB][:, :], f(KX_H[:, :]), ALU.subtract, [t2] + rf[name], "kl")
            free[QB] = [t3]
            tk[name] = [t1, t2, t3]

        def values(g):
            b = g % 2
            _, th, tl, _ = XR[g]
            ts = []
            for a in range(4):
                bk = TB[a // 2]
                o = PS[bk][:, 256 * (a % 2):256 * (a % 2) + 256]
                seq = []
                for dc in range(2):
                    wv = R2[:, 8192:9728].rearrange("p (l n) -> p l n", l=2)[:, :, 512 + 128 * dc:640 + 128 * dc]
                    for s_ in (xh, xl):
                        seq.append((s_[:, b, dc, 128 * a:128 * a + 128], wv))
                mms = [(o, l, r, n == 0, n == 3) for n, (l, r) in enumerate(seq)]
                ts.append(pe("pe_v", free[bk] if a % 2 == 0 else [], mms))
            for z in range(2):
                src = PS[TB[z]][:, :].rearrange("p (t l n) -> p t l n", t=2, l=2)
                t1 = copy("act", R[:, 0, 0:256].rearrange("p (t n) -> p t n", t=2),
                          src[:, :, 1, :], [ts[2 * z + 1]] + rf["r0"])
                rv = R[:, 0, 0:256].rearrange("p (t n) -> p t n", t=2)
                t2 = tt("dve", rv, rv, src[:, :, 0, :], ALU.add, [t1])
                free[TB[z]] = [t2]
                t3 = copy("dve", VH[:, 2 * z:2 * z + 2, :], rv, [t2] + rf["v"], "vh")
                t4 = tt("dve", VL[:, 2 * z:2 * z + 2, :], rv, f(VH[:, 2 * z:2 * z + 2, :]), ALU.subtract,
                        [t3], "vl")
                rf["r0"] = [t4]
            tk["v"] = [t3, t4]

        def weights_of_heads(g):
            ta = XR[g][0]
            mms = [(PS[SB_[0]][:, NH * i:NH * i + NH], xf[:, dc, 128 * i:128 * i + 128], wiw[:, dc, :], dc == 0, dc == 1)
                   for i in range(4) for dc in range(2)]
            t = pe("pe_iw", [ta, t_iw] + free[SB_[0]], mms)
            xn_free[0] = [t, XR[g][2]]
            t = copy("dve", IW[:], PS[SB_[0]][:, 0:64].rearrange("p (t e) -> p t e", e=NH), [t] + rf["iw"])
            free[SB_[0]] = [t]
            tk["iw"] = [t]

        def flip_group(g):
            XR[g] = flip(g, xn, normed[g], SB_, [free[SB_[0]], free[SB_[1]]])
            free[SB_[0]] = free[SB_[1]] = [XR[g][0]]

        bias = {}

        def topk(g):
            pieces = []
            for b in range(2):
                two = [(i, h, I[:, o:o + n], IM[:, o:o + n], W[g % 2][:, o:o + n], n)
                       for i, (bb, h, o, n) in enumerate(TILES) if bb == b]
                tok = {}

                def causal(two=two, tok=tok):
                    for i, h, Is, Ms, Ws, n in two:
                        tok[i] = op("pool", lambda e, Is=Is, Ms=Ms, h=h, n=n: e.affine_select(
                            out=Ms, in_=Is, compare_op=ALU.is_ge, fill=NEG, base=128 * h, pattern=[[-1, n]],
                            channel_multiplier=1), [tk[f"i{i}"]] + rf[f"im{i}"])
                        rf[f"i{i}"] = [tok[i]]

                def best(r, two=two, tok=tok):
                    ts = {}
                    for i, h, Is, Ms, Ws, n in two:
                        src = Ms if r == 0 else Ws
                        ts[i] = op("dve", lambda e, i=i, src=src: e.max(M8[:, i, :], src), [tok[i]])
                    for i, h, Is, Ms, Ws, n in two:
                        src = Ms if r == 0 else Ws
                        tok[i] = op("dve", lambda e, i=i, src=src, Ws=Ws: e.match_replace(Ws, M8[:, i, :], src, MARK),
                                    [ts[i]] + rf[f"w{g % 2}"])

                def mask(two=two, tok=tok):
                    for i, h, Is, Ms, Ws, n in two:
                        tok[i] = op("dve", lambda e, Ws=Ws: e.tensor_scalar(Ws, Ws, MARK, None, ALU.not_equal), [tok[i]])
                    for i, h, Is, Ms, Ws, n in two:
                        tok[i] = op("dve", lambda e, Ws=Ws, Ms=Ms: e.scalar_tensor_tensor(
                            Ws, Ms, NEG / 2, Ws, ALU.is_le, ALU.max), [tok[i]])
                        rf[f"im{i}"] = [tok[i]]
                    for i, h, Is, Ms, Ws, n in two:
                        bias[(g, i)] = op("dve", lambda e, Ws=Ws: e.tensor_scalar(Ws, Ws, NEG, None, ALU.mult), [tok[i]])

                causal()
                pieces += [lambda best=best, r=r: best(r) for r in range(4)] + [mask]
            return pieces

        def head(g, h, wsrc, wtok, F, H, L, wf_, sem, bank=QB):
            b = g % 2
            _, th, tl, _ = XR[g]
            k, i = h // 2, h % 2
            w = wsrc[:, 1024 * k:1024 * k + 1024]
            pairs = [(w[:, 256 * i + 128 * dc:256 * i + 128 * dc + 128],
                      w[:, 512 + 256 * i + 128 * dc:512 + 256 * i + 128 * dc + 128],
                      xh[:, b, dc, :], xl[:, b, dc, :]) for dc in range(2)]
            t = pe(sem, [th, tl, wtok[k]] + free[bank], three(PS[bank][:, :], pairs))
            p2 = PS[bank][:, :].rearrange("p (b z n) -> p b z n", b=2, z=2)
            t1 = copy("act", F, p2[:, :, 0, :], [t] + rf[wf_], sem + "f")
            t2 = copy("act", H, p2[:, :, 1, :], rf[wf_], sem + "h")
            t3 = tt("dve", L, p2[:, :, 1, :], f(H), ALU.subtract, [t2] + rf[wf_], sem + "l")
            free[bank] = [t3]
            if h == NH - 1 and sem == "pe_q":
                xbuf_free[b] = [t]
            return [t1, t2, t3]

        def products(bank, b, F, H, L, KXF, KXH, KXL, waits, sem):
            o = PS[bank]
            kb = slice(256 * b, 256 * b + 256)
            mms = [(o[:, 0:128], F[:, b, :], KXF[:, b, :], True, True)]
            mms += three(o[:, 128:384], [(H[:, b, :], L[:, b, :], KXH[:, kb], KXL[:, kb])])
            return pe(sem, waits + free[bank], mms)

        def qi_of(g, h):
            if g == 0:
                r = h % 4
                return QF[:, r, :, :], QH[:, r, :, :], QL[:, r, :, :], f"q{r}"
            return QIF, QIH, QIL, "qi"

        def idx_project(g, h):
            F, H, L, name = qi_of(g, h)
            tk[f"qi{h}"] = head(g, h, R2, t_wqi, F[:, :, :], H[:, :, :], L[:, :, :], name, "pe_qi",
                                (QB, OB)[h % 2] if g == 0 else QB)

        def idx_logits(g, h):
            F, H, L, name = qi_of(g, h)
            for b in range(2):
                t = products(SB_[b], b, F, H, L, KIF, KIH, KIL, tk[f"qi{h}"] + tk["ki"], "pe_l")
                tr = op("act", lambda e, b=b: e.activation(R[:, b, :], PS[SB_[b]][:, 0:384], ACT.Relu),
                        [t] + rf[f"r{b}"], "relu")
                free[SB_[b]] = [tr]
                for z in range(2):
                    i = 2 * b + z
                    o, n = 384 * b + 128 * z, 128 * (z + 1)
                    r, Is, iw = R[:, b, 128 * z:128 * z + n], I[:, o:o + n], IW[:, i, h:h + 1]
                    if h == 0:
                        ta = op("dve", lambda e, r=r, Is=Is, iw=iw: e.tensor_scalar(Is, r, iw, None, ALU.mult),
                                [tr, *tk["iw"]] + rf[f"i{i}"], "acc")
                    else:
                        ta = op("dve", lambda e, r=r, Is=Is, iw=iw: e.scalar_tensor_tensor(
                            Is, r, iw, Is, ALU.mult, ALU.add), [tr, tk[f"i{i}"]], "acc")
                    tk[f"i{i}"] = ta
                rf[f"r{b}"] = [ta]
            rf[name] = [t]
            if h == NH - 1:
                rf["ki"] = [t]
                rf["iw"] = [ta]

        qt = {}
        SMT, PTT, OT, YT = {}, {}, {}, {}

        def main_project(U):
            g, u = divmod(U, 16)
            r = u % 4
            qt[U] = head(g, u, R1, t_wq, QF[:, r, :, :], QH[:, r, :, :], QL[:, r, :, :], f"q{r}", "pe_q")

        def scores(U):
            g, u = divmod(U, 16)
            j, b = divmod(u, 2)
            k = U % 2
            tn = []
            for i in range(2):
                h = 2 * j + i
                r = h % 4
                t = products(SB_[i], b, QF[:, r, :, :], QH[:, r, :, :], QL[:, r, :, :], KF, KH, KL,
                             qt[16 * g + h] + tk["k"], "pe_s")
                if b == 1:
                    rf[f"q{r}"] = [t]
                for z in range(2):
                    n, o = 128 * (z + 1), 128 * z
                    tm = op("dve", lambda e, i=i, z=z, n=n, o=o, k=k, b=b, g=g: e.tensor_tensor_reduce(
                        out=SP[:, k, i, o:o + n], in0=PS[SB_[i]][:, o:o + n], in1=W[g % 2][:, 384 * b + o:384 * b + o + n],
                        scale=1.0, scalar=-3e38, op0=ALU.add, op1=ALU.max, accum_out=MX[:, k, 2 * i + z:2 * i + z + 1]),
                        [t, bias[(g, 2 * b + z)]] + rf[f"sp{k}"], "mask")
                free[SB_[i]] = [tm]
                tn.append(op("dve", lambda e, k=k, i=i: e.tensor_scalar(
                    NB[:, k, 2 * i:2 * i + 2], MX[:, k, 2 * i:2 * i + 2], -SCALE, None, ALU.mult), [tm], "nb"))
            for i in range(2):
                for z in range(2):
                    n, o = 128 * (z + 1), 128 * z
                    te = op("act", lambda e, i=i, z=z, n=n, o=o, k=k: e.activation(
                        SP[:, k, i, o:o + n], SP[:, k, i, o:o + n], ACT.Exp, scale=SCALE,
                        bias=NB[:, k, 2 * i + z:2 * i + z + 1], accum_out=SM[:, k, 2 * i + z:2 * i + z + 1]),
                        [tn[i]], "exp")
            SMT[U] = te
            if u == 15:
                rf["k"] = [t]
                rf[f"w{g % 2}"] = [tm]

        def normalise(U):
            k = U % 2
            busy = U % 16 in (14, 15, 0) and 0 < U < 62 or U == 0
            t = op("dve", lambda e, k=k: e.reciprocal(RC[:, k, :], SM[:, k, :]), [SMT[U]], "rc")
            ts = {}
            for i in range(2):
                for z in range(2):
                    n, o = 128 * (z + 1), 128 * z
                    eng = "pool" if busy and i == 0 else "dve"
                    ts[eng] = op(eng, lambda e, i=i, z=z, n=n, o=o, k=k: e.tensor_scalar(
                        SP[:, k, i, o:o + n], SP[:, k, i, o:o + n], RC[:, k, 2 * i + z:2 * i + z + 1], None, ALU.mult),
                        [t], "pn_" + eng)
            SMT[U] = list(ts.values())

        def flip_p(U):
            k = U % 2
            for i in range(2):
                o = PS[TB[i]]
                srcs = [SP[:, k, i, 0:128], SP[:, k, i, 128:256], SP[:, k, i, 256:384]]
                for z, s_ in enumerate(srcs):
                    fn = lambda e, o=o, z=z, s_=s_: e.transpose(o[:, 128 * z:128 * z + 128], s_, ident)
                    w = SMT[U] + free[TB[i]] if z == 0 else []
                    if z == 2:
                        t = op("pe", fn, w, "pe_t")
                    else:
                        quiet("pe", fn, w)
                th = copy("act", PTH[:, i, :], o[:, 0:384], [t] + rf["pt"], "pth")
                tl = tt("dve", PTL[:, i, :], o[:, 0:384], f(PTH[:, i, :]), ALU.subtract, [th] + rf["pt"], "ptl")
                free[TB[i]] = [tl]
            rf[f"sp{k}"] = [t]
            PTT[U] = [th, tl]

        def pv(U):
            g, u = divmod(U, 16)
            b = u % 2
            o = PS[OB]
            o2 = o[:, :].rearrange("p (h n) -> p h n", h=2)
            mms = []
            mms += three(o2[:, :, :], [(VH[:, 2 * b, :], VL[:, 2 * b, :], PTH[:, :, 0:256], PTL[:, :, 0:256])],
                         True, False)
            mms += three(o2[:, :, 128:256], [(VH[:, 2 * b + 1, :], VL[:, 2 * b + 1, :],
                                              PTH[:, :, 256:384], PTL[:, :, 256:384])], False, True)
            t = pe("pe_o", PTT[U] + tk[f"v_{g}"] + free[OB], mms)
            rf["pt"] = [t]
            if u == 15:
                rf["v"] = [t]
            th = copy("act", OH, o[:, :], [t] + rf["o"], "oh")
            tl = tt("dve", OL, o[:, :], f(OH), ALU.subtract, [th], "ol")
            free[OB] = [tl]
            OT[U] = [th, tl]

        outs = []

        def wo(U):
            g, u = divmod(U, 16)
            j, b = divmod(u, 2)
            bank = YB[b]
            first = True
            for i in range(2):
                h = 2 * j + i
                w = R1[:, 8192 + 1024 * (h // 2):8192 + 1024 * (h // 2) + 1024]
                wh, wl = w[:, 256 * (h % 2):256 * (h % 2) + 256], w[:, 512 + 256 * (h % 2):512 + 256 * (h % 2) + 256]
                for z in range(2):
                    sl = slice(256 * i + 128 * z, 256 * i + 128 * z + 128)
                    y = PS[bank][:, 256 * z:256 * z + 256]
                    mms = [(y, OH[:, sl], wh), (y, OH[:, sl], wl), (y, OL[:, sl], wh)]
                    mms = [(*m, j == 0 and i == 0 and z == 0 and q == 0, j == 7 and i == 1 and q == 2)
                           for q, m in enumerate(mms)]
                    wts = OT[U] + [t_wo[h // 2]] if i == 0 and z == 0 else []
                    if j == 0 and first:
                        wts = wts + free[bank]
                    first = False
                    t = pe("pe_y", wts, mms)
            rf["o"] = [t]
            if j == 7:
                xs = X[:, 4 * g + 2 * b:4 * g + 2 * b + 2, :]
                y = PS[bank][:, :].rearrange("p (t d) -> p t d", d=D)
                tx = tt("dve", xs, xs, y, ALU.add, [t], "xres")
                free[bank] = [tx]
                xres[g] = tx

        def store(g, t):
            outs.append(load(out[512 * g:512 * g + 512, :].rearrange("(t p) d -> p t d", p=128),
                             X[:, 4 * g:4 * g + 4, :], [t], f"out{g}"))

        slots2 = [R2[:, 1536 * i:1536 * i + 1536] for i in range(3)]
        wt2, experts2 = [], []

        def shared2(i, waits):
            wt2.append(weight(wsh_in[i], 768, slots2[i], waits, "pool", "pool"))

        def expert2(e, p, waits, eh="pool", el="pool"):
            src, w, dst = part(e, p, 1)
            experts2.append(weight(src, w, dst, waits, eh, el))

        project(0, 0)
        weights_of_heads(0)
        idx_project(0, 0)
        for h in range(NH):
            if h + 1 < NH:
                idx_project(0, h + 1)
            idx_logits(0, h)
            if h == 3:
                normed[1] = centre(1, 4, late["moments"], xn, xn_free[0], "dve")
            if h == 8:
                flip_group(1)
        pend = topk(0)

        def drip(n):
            for _ in range(min(n, len(pend))):
                pend.pop(0)()

        def begin_idx(g):
            project(0, g)
            weights_of_heads(g)

        begin_idx(1)
        drip(1)
        idx_project(1, 0)
        drip(1)
        main_project(0)
        drip(2)
        idx_logits(1, 0)
        main_project(1)
        idx_project(1, 1)
        drip(3)
        idx_logits(1, 1)
        nextq = [2]

        def ahead_to(U):
            while nextq[0] <= min(U, 63):
                main_project(nextq[0])
                nextq[0] += 1

        for U in range(64):
            g, u = divmod(U, 16)
            V = U + 18
            gi, hi = divmod(V, 16)
            idx = gi < NG
            if u == 0:
                project(1, g)
            if 0 < u < 14 and idx:
                idx_project(gi, hi)
            if u == 1:
                drip(9)
            if u == 0:
                if U:
                    wo(U - 3)
                    pv(U - 2)
                    flip_p(U - 1)
                drip(1)
                if idx and U:
                    idx_logits(gi, 1)
                if idx:
                    idx_project(gi, 2)
                scores(U)
                drip(1)
                ahead_to(U + 2 if idx else U + 3)
                normalise(U)
                drip(1)
                if idx:
                    idx_logits(gi, 2)
            elif idx and u in (14, 15):
                scores(U)
                wo(U - 3)
                if u == 14:
                    begin_idx(gi)
                else:
                    idx_logits(gi, 0)
                drip(1)
                ahead_to(U + 2)
                normalise(U)
                pv(U - 2)
                drip(1)
                flip_p(U - 1)
                idx_project(gi, hi)
                drip(1)
            else:
                scores(U)
                if U >= 3:
                    wo(U - 3)
                if idx:
                    idx_logits(gi, hi)
                    drip(1)
                    ahead_to(U + 2)
                    normalise(U)
                if U >= 2:
                    pv(U - 2)
                drip(1)
                if u == 1:
                    values(g)
                    tk[f"v_{g}"] = tk["v"]
                flip_p(U - 1)
                if not idx:
                    ahead_to(U + 3)
                    normalise(U)
                drip(1)
            if u == 8 and g + 2 < NG:
                do_norm(g + 2)
            if u == 13:
                if g + 1 < NG:
                    pend = topk(g + 1)
                if g + 2 < NG:
                    flip_group(g + 2)
                if g == NG - 2:
                    r2_edge = [(s, count[s]) for s in ("pe_qi", "pe_k", "pe_v")]
            if g == NG - 1:
                if 1 <= u < 15:
                    r2 = [*r2_edge, ("pe_k", count["pe_k"]), ("pe_v", count["pe_v"])]
                    if u % 2 == 1:
                        if u < 6:
                            shared2(u // 2, r2)
                        else:
                            expert2((u - 7) // 4, (u - 7) // 2 % 2, r2)
                if u == 2:
                    m = Moe(1, PA, lambda g: [xres[g]], store, free, [last_of[e] for e in ("pe", "act", "dve", "pool")],
                            xn_free[0])
                    m.norm(0)
                elif u == 4:
                    m.flip(0)
                elif u == 5:
                    m.logits(0)
                    m.norm(1)
                elif u == 6:
                    m.halves(0)
                elif u == 7:
                    m.flip(1)
                elif u == 8:
                    m.logits(1)
                elif u == 10:
                    m.norm(2)
                elif u == 12:
                    m.choose(0)
                elif u == 13:
                    m.count(0)
                    m.halves(1)
                    q_edge = [("pe_q", count["pe_q"])]
                    expert2(2, 0, q_edge)
                elif u == 14:
                    m.flip(2)
                    expert2(2, 1, q_edge)
                    expert2(3, 0, q_edge)
                elif u == 15:
                    expert2(3, 1, q_edge)
        for U in (64, 65, 66):
            wo(U - 3)
            if U < 66:
                pv(U - 2)
            if U < 65:
                flip_p(U - 1)
                m.place(0)
                scatters(m, 0)
            elif U == 65:
                m.logits(2)
        fs.close()
        edge2 = [last_of[e] for e in ("pe", "act", "dve")]

        fs = ExitStack()
        m.settle(sb("FA", [128, 4352], f32, fs), sb("RA", [128, 3072], f32r, fs), edge2)
        parts = [(e, p) for e in range(4, NE) for p in range(2)]
        brought = {}

        def ahead2(i):
            for q in parts[2 * i - 2:2 * i] if i else []:
                experts2.append(split(brought.pop(q), *part(*q, 1)[1:], q_edge if q[0] < 5 else edge2))
            for q in parts[2 * i:2 * i + 2]:
                brought[q] = bring(*part(*q, 1)[:2])

        prep = [[lambda: m.norm(3)], [], [], [lambda: m.halves(2), lambda: m.load_slots(0)], [lambda: m.flip(3)],
                [lambda: m.turn_ids(0), m.prefetch, lambda: m.logits(3)], [lambda: m.halves(3)], []]
        m.shared([0, 1], slots2, wt2, [filler(*p, lambda i=i: ahead2(i)) for i, p in enumerate(prep)])
        m.experts = experts2
        fill2 = routing_fills(m)
        fill2 |= {0: [lambda: m.choose(1)], 1: [lambda: m.count(1)], 2: [lambda: m.place(1), *fill2[2]]}
        m.sparse([filler(*fill2.get(i, [])) for i in range(48)])
        m.shared([2, 3], slots2, wt2, [lambda i=i: m.collect(1, i) for i in range(8)])
        m.add()
        fs.close()

        sems = {s: ctx.enter_context(nc.semaphore(f"s_{s}")) for s in count}
        block = ctx.enter_context(nc.Block())

        def run(e, name):
            seen = {}
            for fn, waits, sem, inc in prog[name]:
                for s, v in waits:
                    if seen.get(s, 0) < v:
                        e.wait_ge(sems[s], v)
                        seen[s] = v
                ins = fn(e)
                if sem is not None:
                    ins.then_inc(sems[sem], inc)

        @block.tensor
        def _(e):
            run(e, "pe")

        @block.scalar
        def _(e):
            run(e, "act")

        @block.vector
        def _(e):
            run(e, "dve")

        @block.gpsimd
        def _(e):
            run(e, "pool")

        @block.sync
        def _(e):
            run(e, "sp")
            for s, v in outs:
                e.wait_ge(sems[s], v)


def kernel(**inputs):
    import numpy as _np
    import concourse.bacc as _bacc
    from concourse import mybir as _mybir
    from concourse.bass_utils import run_bass_kernel_spmd as _run

    a = {k[3:]: _np.asarray(v) for k, v in inputs.items()}

    def halves(w):
        return w.reshape(2, 128, w.shape[1]).transpose(1, 0, 2)

    def shared(w):
        w = _np.concatenate([w, _np.zeros((D, 32), w.dtype)], axis=1)
        return halves(w).reshape(128, 2, 3, 128).transpose(2, 0, 1, 3).reshape(3, 128, 256)

    down = _np.concatenate([a["ffn_sw_down"], _np.zeros((32, D), a["ffn_sw_down"].dtype)], axis=0).reshape(3, 128, D)
    wsh = _np.concatenate([shared(a["ffn_sw_gate"]), shared(a["ffn_sw_up"]), down], axis=2)

    def by_pairs(w):
        return halves(w).reshape(128, 2, 8, 2, 128).transpose(2, 0, 3, 1, 4).reshape(8, 128, 512)

    gu = _np.concatenate([a["ffn_w_gate"], a["ffn_w_up"]], axis=2).reshape(NE, 2, 128, 2 * HE)
    gu = gu.transpose(0, 2, 1, 3).reshape(NE, 128, 4 * HE)
    dn = a["ffn_w_down"].reshape(NE, 2, 88, D).transpose(0, 2, 1, 3).reshape(NE, 88, 2 * D)
    dn = _np.concatenate([dn, _np.zeros((NE, 40, 2 * D), dn.dtype)], axis=1)
    wex = _np.concatenate([gu, dn], axis=2)
    less = _np.arange(NE)[None, :] < _np.arange(NE)[:, None]
    row = _np.concatenate([_np.repeat(_np.arange(NT), 7), _np.diff(PLACES[0]), _np.diff(PLACES[1]),
                           _np.zeros(9), less.reshape(64)])

    arrays = {
        "x_in": a["attn_x"].reshape(T, D),
        "cst_in": _np.concatenate([_np.eye(128), _np.triu(_np.ones((128, 128)), 1)], axis=1).astype(_np.float32),
        "row_in": _np.broadcast_to(row.astype(_np.float32), (128, 248)),
        "tok_in": _np.arange(T, dtype=_np.float32).reshape(16, 128).T,
        "gw_in": halves(a["ffn_gate_w"]).reshape(128, 2 * NE),
        "wsh_in": wsh,
        "wex_in": wex,
        "wqi_in": by_pairs(a["attn_wq_idx"]),
        "ws_in": _np.concatenate([halves(a[k]).reshape(128, 256) for k in ("attn_wk_idx", "attn_wk", "attn_wv")], axis=1),
        "wiw_in": halves(a["attn_w_iw"]).reshape(128, 2 * NH),
        "wq_in": by_pairs(a["attn_wq"]),
        "wo_in": a["attn_wo"].reshape(8, 2, 128, D).transpose(0, 2, 1, 3).reshape(8, 128, 512),
    }
    nc = _bacc.Bacc("TRN2", target_bir_lowering=False, num_devices=1)
    args = []
    for name in arrays:
        arrays[name] = _np.ascontiguousarray(arrays[name])
        args.append(nc.dram_tensor(name, arrays[name].shape, _mybir.dt.from_np(arrays[name].dtype),
                                   kind="ExternalInput").ap())
    args.append(nc.dram_tensor("out_0", (T, D), _mybir.dt.float32, kind="ExternalOutput").ap())
    macaron_kernel(nc, *args)
    r = _run(nc, [arrays], core_ids=[0])
    return r.results[0]["out_0"].reshape(8, 256, D)
```
